# Optimizing a Trainium2 kernel written in Bass

```python
import numpy as np
import jax
import jax.numpy as jnp

def _softmax(x, axis=-1):
    return jax.nn.softmax(x, axis=axis)

def _gelu(x):
    return jax.nn.gelu(x, approximate=True)

def _silu(x):
    return jax.nn.silu(x)

def _sigmoid(x):
    return jax.nn.sigmoid(x)

def _layernorm(x, axis=-1, eps=1e-05):
    m = jnp.mean(x, axis=axis, keepdims=True)
    v = jnp.var(x, axis=axis, keepdims=True)
    return (x - m) / jnp.sqrt(v + eps)

def _scatter_add(tgt, idx, src, axis=0):
    return tgt.at[idx].add(src)

def _segment_sum(src, seg, n):
    return jax.ops.segment_sum(src, seg, n)
kernel_name = 'mk_adj_resnorm_d2_adj_r2_83e2f4'

def setup_inputs(seed: int=0):
    np.random.seed(seed)
    _w = jnp.asarray

    def _rec_inputs():
        import jax
        import jax.numpy as jnp
        _gk = jax.random.key(seed)
        x = -0.0001538 + 1 * jax.random.normal(jax.random.fold_in(_gk, 1), (16, 512, 384), jnp.float32)
        _a = jax.random.bernoulli(jax.random.fold_in(_gk, 2), 0.0078125, (16, 512, 512))
        _a = jnp.logical_or(_a, jnp.swapaxes(_a, -1, -2))
        _a = jnp.logical_or(_a, jnp.eye(512, dtype=bool))
        _af = _a.astype(jnp.float32)
        _af = _af * jax.random.uniform(jax.random.fold_in(_gk, 3), (16, 512, 512), jnp.float32, 0.05, 5.06092)
        adj = _af
        return (x, adj)
    x, adj = _rec_inputs()

    def _L0_gnn_setup():
        import jax, jax.numpy as jnp
        import numpy as np
        D_MODEL = 384
        NHEADS = 8
        D_FF = 1536
        B, N = (8, 512)
        EPS = 1e-06

        def _rmsnorm(x, alpha, gamma):
            x = x * jax.lax.rsqrt(jnp.mean(x * x, axis=-1, keepdims=True) + EPS)
            return alpha * x + gamma
        key = jax.random.key(seed)
        ks = jax.random.split(key, 10)
        d, f = (D_MODEL, D_FF)
        s = 1.0 / np.sqrt(d)
        inp = {'x': jax.random.normal(ks[0], (B, N, d), dtype=jnp.float32), 'attn_bias': jax.random.normal(ks[1], (B, N, N), dtype=jnp.float32), 'wq': jax.random.normal(ks[2], (d, d), dtype=jnp.float32) * s, 'bq': jnp.zeros((d,), jnp.float32), 'wk': jax.random.normal(ks[3], (d, d), dtype=jnp.float32) * s, 'bk': jnp.zeros((d,), jnp.float32), 'wv': jax.random.normal(ks[4], (d, d), dtype=jnp.float32) * s, 'bv': jnp.zeros((d,), jnp.float32), 'wo': jax.random.normal(ks[5], (d, d), dtype=jnp.float32) * s, 'bo': jnp.zeros((d,), jnp.float32), 'w1': jax.random.normal(ks[6], (d, f), dtype=jnp.float32) * s, 'b1': jnp.zeros((f,), jnp.float32), 'w2': jax.random.normal(ks[7], (f, d), dtype=jnp.float32) * (1.0 / np.sqrt(f)), 'b2': jnp.zeros((d,), jnp.float32), 'alpha1': jnp.ones((d,), jnp.float32), 'gamma1': jnp.ones((d,), jnp.float32), 'alpha2': jnp.ones((d,), jnp.float32), 'gamma2': jnp.ones((d,), jnp.float32)}
        return inp
    _L0_gnn_all = _L0_gnn_setup()
    _L0_gnn_in = {k: v for k, v in _L0_gnn_all.items() if k in ('wq', 'bq', 'wk', 'bk', 'wv', 'bv', 'wo', 'bo', 'w1', 'b1', 'w2', 'b2', 'alpha1', 'gamma1', 'alpha2', 'gamma2')}
    del _L0_gnn_all

    def _L1_gnn_setup():
        import jax, jax.numpy as jnp
        import numpy as np
        NUM_HEADS = 12
        HIDDEN = 384
        HEAD = HIDDEN // NUM_HEADS
        B, N = (16, 256)
        key = jax.random.key(seed)
        ks = jax.random.split(key, 9)
        s = 0.02
        return {'x': jax.random.normal(ks[0], (B, N, HIDDEN), jnp.float32), 'spatial_encoding': jax.random.normal(ks[1], (B, N, N), jnp.float32), 'edge_encoding': jax.random.normal(ks[2], (B, N, N), jnp.float32), 'Wq': jax.random.normal(ks[3], (HIDDEN, HIDDEN), jnp.float32) * s, 'Wk': jax.random.normal(ks[4], (HIDDEN, HIDDEN), jnp.float32) * s, 'Wv': jax.random.normal(ks[5], (HIDDEN, HIDDEN), jnp.float32) * s, 'bv': jax.random.normal(ks[6], (HIDDEN,), jnp.float32) * s, 'Wo': jax.random.normal(ks[7], (HIDDEN, HIDDEN), jnp.float32) * s, 'bo': jax.random.normal(ks[8], (HIDDEN,), jnp.float32) * s}
    _L1_gnn_all = _L1_gnn_setup()
    _L1_gnn_in = {k: v for k, v in _L1_gnn_all.items() if k in ('Wq', 'Wk', 'Wv', 'bv', 'Wo', 'bo')}
    del _L1_gnn_all
    return {'x': x, 'adj': adj, 'L0_gnn_wq': _L0_gnn_in['wq'], 'L0_gnn_bq': _L0_gnn_in['bq'], 'L0_gnn_wk': _L0_gnn_in['wk'], 'L0_gnn_bk': _L0_gnn_in['bk'], 'L0_gnn_wv': _L0_gnn_in['wv'], 'L0_gnn_bv': _L0_gnn_in['bv'], 'L0_gnn_wo': _L0_gnn_in['wo'], 'L0_gnn_bo': _L0_gnn_in['bo'], 'L0_gnn_w1': _L0_gnn_in['w1'], 'L0_gnn_b1': _L0_gnn_in['b1'], 'L0_gnn_w2': _L0_gnn_in['w2'], 'L0_gnn_b2': _L0_gnn_in['b2'], 'L0_gnn_alpha1': _L0_gnn_in['alpha1'], 'L0_gnn_gamma1': _L0_gnn_in['gamma1'], 'L0_gnn_alpha2': _L0_gnn_in['alpha2'], 'L0_gnn_gamma2': _L0_gnn_in['gamma2'], 'L1_gnn_Wq': _L1_gnn_in['Wq'], 'L1_gnn_Wk': _L1_gnn_in['Wk'], 'L1_gnn_Wv': _L1_gnn_in['Wv'], 'L1_gnn_bv': _L1_gnn_in['bv'], 'L1_gnn_Wo': _L1_gnn_in['Wo'], 'L1_gnn_bo': _L1_gnn_in['bo']}

def reference(x, adj, L0_gnn_wq, L0_gnn_bq, L0_gnn_wk, L0_gnn_bk, L0_gnn_wv, L0_gnn_bv, L0_gnn_wo, L0_gnn_bo, L0_gnn_w1, L0_gnn_b1, L0_gnn_w2, L0_gnn_b2, L0_gnn_alpha1, L0_gnn_gamma1, L0_gnn_alpha2, L0_gnn_gamma2, L1_gnn_Wq, L1_gnn_Wk, L1_gnn_Wv, L1_gnn_bv, L1_gnn_Wo, L1_gnn_bo):
    import jax
    import jax.numpy as jnp

    def _L0_gnn_ref(x, attn_bias, wq, bq, wk, bk, wv, bv, wo, bo, w1, b1, w2, b2, alpha1, gamma1, alpha2, gamma2):
        import jax, jax.numpy as jnp
        import numpy as np
        D_MODEL = 384
        NHEADS = 8
        D_FF = 1536
        B, N = (8, 512)
        EPS = 1e-06

        def _rmsnorm(x, alpha, gamma):
            x = x * jax.lax.rsqrt(jnp.mean(x * x, axis=-1, keepdims=True) + EPS)
            return alpha * x + gamma
        b, n, d = x.shape
        h = NHEADS
        dh = d // h
        scaling = dh ** (-0.5)

        def split_heads(t):
            return t.reshape(b, n, h, dh).transpose(0, 2, 1, 3)
        q = split_heads(x @ wq + bq)
        k = split_heads(x @ wk + bk)
        v = split_heads(x @ wv + bv)
        scores = jnp.einsum('bhqd,bhkd->bhqk', q, k) * scaling
        scores = scores + attn_bias[:, None, :, :]
        attn = jax.nn.softmax(scores, axis=-1)
        ctx = jnp.einsum('bhij,bhjd->bhid', attn, v)
        ctx = ctx.transpose(0, 2, 1, 3).reshape(b, n, d)
        attn_out = ctx @ wo + bo
        x = _rmsnorm(x + attn_out, alpha1, gamma1)
        ff = jax.nn.silu(x @ w1 + b1) @ w2 + b2
        x = _rmsnorm(x + ff, alpha2, gamma2)
        return x

    def _L1_gnn_ref(x, spatial_encoding, edge_encoding, Wq, Wk, Wv, bv, Wo, bo):
        import jax, jax.numpy as jnp
        import numpy as np
        NUM_HEADS = 12
        HIDDEN = 384
        HEAD = HIDDEN // NUM_HEADS
        B, N = (16, 256)
        b, n, h = x.shape
        scale = jnp.asarray(HIDDEN, x.dtype) ** (-0.5)
        q = (x @ Wq.T).reshape(b, n, NUM_HEADS, HEAD)
        k = (x @ Wk.T).reshape(b, n, NUM_HEADS, HEAD)
        v = (x @ Wv.T + bv).reshape(b, n, NUM_HEADS, HEAD)
        bias = (spatial_encoding + edge_encoding)[:, None]
        scores = jnp.einsum('bqhd,bkhd->bhqk', q, k) * scale + bias
        row_nonzero = jnp.any(scores != 0, axis=-1, keepdims=True)
        scores = jnp.where(row_nonzero, scores, -jnp.inf)
        p = jax.nn.softmax(scores, axis=-1)
        p = jnp.nan_to_num(p)
        out = jnp.einsum('bhqk,bkhd->bqhd', p, v).reshape(b, n, h)
        return out @ Wo.T + bo
    x = _layernorm(x + _L0_gnn_ref(x, adj, L0_gnn_wq, L0_gnn_bq, L0_gnn_wk, L0_gnn_bk, L0_gnn_wv, L0_gnn_bv, L0_gnn_wo, L0_gnn_bo, L0_gnn_w1, L0_gnn_b1, L0_gnn_w2, L0_gnn_b2, L0_gnn_alpha1, L0_gnn_gamma1, L0_gnn_alpha2, L0_gnn_gamma2), axis=-1)
    x = _layernorm(x + _L1_gnn_ref(x, adj, adj, L1_gnn_Wq, L1_gnn_Wk, L1_gnn_Wv, L1_gnn_bv, L1_gnn_Wo, L1_gnn_bo), axis=-1)
    return x

_drawn_inputs = setup_inputs


def setup_inputs(seed=0):
    import zlib

    import numpy as np

    out = dict(_drawn_inputs(seed))
    spreads = {'L0_gnn_bq': (0.0, 0.8),
     'L0_gnn_bk': (0.0, 0.8),
     'L0_gnn_bv': (0.0, 0.1),
     'L0_gnn_bo': (0.0, 0.1),
     'L0_gnn_b1': (0.0, 0.34),
     'L0_gnn_b2': (0.0, 0.1),
     'L0_gnn_alpha1': (1.0, 0.2),
     'L0_gnn_gamma1': (1.0, 0.2),
     'L0_gnn_alpha2': (1.0, 0.2),
     'L0_gnn_gamma2': (1.0, 0.2)}
    factors = {'L1_gnn_Wq': 8.0, 'L1_gnn_Wk': 8.0, 'L1_gnn_bv': 6.312, 'L1_gnn_bo': 2.998}
    for name, (base, spread) in spreads.items():
        noise = np.random.default_rng([zlib.crc32(name.encode()), seed]).standard_normal(out[name].shape)
        drawn = base * np.exp(spread * noise) if base else spread * noise
        out[name] = jnp.asarray(drawn.astype(out[name].dtype))
    for name, factor in factors.items():
        out[name] = (out[name] * factor).astype(out[name].dtype)
    return out
```

```python
from contextlib import ExitStack

import concourse.bass as bass
from concourse import mybir

P = 128
ALU = mybir.AluOpType
ACT = mybir.ActivationFunctionType
AX = mybir.AxisListType
F32 = mybir.dt.float32
F32R = mybir.dt.float32r
RMS_EPS = 1e-6
LN_EPS = 1e-5


class Layer:

    def __init__(self, name, heads, dim, passes, adj_factor, rms, guard):
        self.name, self.H, self.dh, self.passes = name, heads, dim, passes
        self.adj_factor, self.rms, self.guard = adj_factor, rms, guard
        D = heads * dim
        self.rows = 2 * dim if passes == 2 else 4 * dim
        self.lo_at = 64 if dim > 32 else 32
        self.per_tile = 2 if dim > 32 else 4
        self.row_step = P // self.per_tile
        self.NT = heads // self.per_tile
        self.v_halves_added = passes == 2
        self.wo_pieces = [(h // self.per_tile, (h % self.per_tile) * self.row_step, dim, h * dim) for h in range(heads)]
        self.tile_dims = P // heads if passes == 2 else dim
        self.tile_heads = P // self.tile_dims
        if passes == 2:
            self.q_to = [(0, 0, 0), (1, 0, dim)]
            self.k_to = [(0, 1, 0), (1, 1, dim), (1, 2, 0), (0, 2, dim)]
        else:
            self.q_to = [(0, 0, 0), (0, 0, dim), (1, 0, 2 * dim), (1, 0, 3 * dim)]
            self.k_to = [(0, 1, 0), (1, 1, dim), (0, 1, 2 * dim), (1, 1, 3 * dim)]
        self.stacks = 1 + len({s for _, s, _ in self.k_to})

    def ctx_rows(self, head):
        row = (head % self.per_tile) * self.row_step
        return row, row + self.dh


def attention_layer(nc, L, x, adj, w, ident_d, out):
    B, N, D = x.shape
    H, dh, NT, M3, QT = L.H, L.dh, L.NT, D // P, N // P
    SCALE = (float(dh) ** -0.5) if L.rms else (float(D) ** -0.5)
    q_scale = SCALE / L.adj_factor
    HALF = QT // 2

    XT, QK, VV, SS = 0, M3, M3 + 2 * M3, M3 + 2 * M3 + QT
    OO = SS + QT * H
    R = OO + QT
    RING = 3

    def prior(n):
        if n >= RING:
            return n - RING
        return max(m for m in range(R) if m % RING == n) - R

    n_copies = [16 * len(to) for to in (L.q_to, L.k_to)]

    PR = 6
    NR = 5

    with ExitStack() as ctx:
        def sb(name, shape, dt=F32):
            return ctx.enter_context(nc.sbuf_tensor(f"{L.name}_{name}", shape, dt))

        def sem(name):
            return ctx.enter_context(nc.semaphore(f"{L.name}_{name}"))

        wq_h, wk_h, wv_h = (sb(n, [P, M3, D], F32R) for n in ("wq_h", "wk_h", "wv_h"))
        wq_l, wk_l, wv_l = (sb(n, [P, M3, D], F32R) for n in ("wq_l", "wk_l", "wv_l"))
        wo_h, wo_l = sb("wo_h", [P, NT, D], F32R), sb("wo_l", [P, NT, D], F32R)
        bq, bk = sb("bq", [P, M3]), sb("bk", [P, M3])
        bv_row, bo_row = sb("bv_row", [P, D]), sb("bo_row", [P, D])
        al_row, ga_row = (sb("al_row", [P, D]), sb("ga_row", [P, D])) if L.rms else (None, None)
        ident = sb("ident", [P, P])
        minus_half = sb("minus_half", [P, QT])
        adj_sb = sb("adj", [P, QT, N])
        x_in = sb("x_in", [P, QT, D])
        at_h, at_l = sb("at_h", [P, 4, N], F32R), sb("at_l", [P, 4, N], F32R)
        ctx_f = sb("ctx_f", [P, 4, N])
        q_places = 2 if L.guard else 1
        q_half = sb("q_half", [P, q_places, 2, N], F32R)
        k_half = sb("k_half", [P, 2, N], F32R)
        if L.guard:
            k_sum, head_mask = sb("k_sum", [P, M3]), sb("head_mask", [P, L.tile_heads])
            k_sum_h, k_sum_l = (sb(n, [P, M3, L.tile_heads], F32R) for n in ("k_sum_h", "k_sum_l"))
            adj_sum, sum_nonzero = sb("adj_sum", [P, QT]), sb("sum_nonzero", [P, QT, H])
        stack = sb("stack", [P, L.stacks, H, N], F32R)
        v_f = sb("v_f", [P, 2, D])
        v_hl = sb("v_hl", [P, QT, H, 2 * L.lo_at], F32R)
        probs = sb("probs", [P, PR, N])
        neg_s = sb("neg_s", [P, NR, N])
        neg_max, row_sum, row_inv, row_keep = (sb(n, [P, 2, QT]) for n in ("neg_max", "row_sum", "row_inv", "row_keep"))
        pt_h, pt_l = sb("pt_h", [P, QT, N], F32R), sb("pt_l", [P, QT, N], F32R)
        ctx_lo = sb("ctx_lo", [dh, N])
        y = sb("y", [P, QT, D])
        stat = sb("stat", [P, QT, 6])
        mean_var = sb("mean_var", [P, QT, 2])
        spread, rstd = sb("spread", [P, QT]), sb("rstd", [P, QT])

        ring = ctx.enter_context(nc.psum_tensor(f"{L.name}_ring", [P, RING, N], F32))
        pt_ps = ctx.enter_context(nc.psum_tensor(f"{L.name}_pt_ps", [P, 2, QT, HALF * P], F32))
        pv_ps = ctx.enter_context(nc.psum_tensor(f"{L.name}_pv_ps", [P, N], F32))

        const_in, consts_set, w_hi, w_lo, bias_set = (sem(n) for n in ("const_in", "consts_set", "w_hi", "w_lo", "bias_set"))
        norm_begun, sum_begun = sem("norm_begun"), sem("sum_begun")
        x_loaded, adj_loaded, x_kept = sem("x_loaded"), sem("adj_loaded"), sem("x_kept")
        bank_full = sem("bank_full")
        xt_hi, xt_lo = sem("xt_hi"), sem("xt_lo")
        qk_hi, qk_lo = sem("qk_hi"), sem("qk_lo")
        q_copied, k_copied = sem("q_copied"), sem("k_copied")
        v_sum, v_hi, v_lo = sem("v_sum"), sem("v_hi"), sem("v_lo")
        k_summed, k_sum_hi, k_sum_split, score_sums, adj_summed, sums_tested = (
            sem(n) for n in ("k_summed", "k_sum_hi", "k_sum_split", "score_sums", "adj_summed", "sums_tested"))
        s_ready, p_exp, keep_ready, inv_ready, p_norm = (sem(n) for n in ("s_ready", "p_exp", "keep_ready", "inv_ready", "p_norm"))
        pt_full, pt_hi, pt_lo = sem("pt_full"), sem("pt_hi"), sem("pt_lo")
        pv_full, ctx_part, ctx_done = sem("pv_full"), sem("ctx_part"), sem("ctx_done")
        ctx_hi, ctx_lo_done = sem("ctx_hi"), sem("ctx_lo_done")
        y_bias, y_res, y_stat, spread_made, rstd_ready, y_scaled, y_ready, y_stored = (
            sem(n) for n in ("y_bias", "y_res", "y_stat", "spread_made", "rstd_ready", "y_scaled", "y_ready", "y_stored"))
        block = ctx.enter_context(nc.Block())

        def staged(ap, tiles):
            return ap.rearrange("p a b -> p (a b)")[:, 0:tiles * D].rearrange("p (a b) -> p a b", a=tiles)

        raw = {"wq": staged(probs[:, 0:3], M3), "wk": staged(probs[:, 3:6], M3), "wv": staged(y[:], M3),
               "wo": staged(ctx_f[:], NT)}
        by_head = lambda ap: ap.rearrange("p (h d) -> p h d", h=H)
        v_his = [v_hl[:, t, :, 0:dh] for t in range(QT)]
        v_los = [v_hl[:, t, :, L.lo_at:L.lo_at + dh] for t in range(QT)]
        n_const = 3 + len(L.wo_pieces) + 3 + (4 if L.rms else 0) + (1 if L.guard else 0)
        halves = [("wq", wq_h, wq_l), ("wk", wk_h, wk_l), ("wv", wv_h, wv_l), ("wo", wo_h, wo_l)]
        x_t = x.rearrange("b (t p) d -> b p t d", p=P)
        adj_t = adj.rearrange("b (t p) n -> b p t n", p=P)
        out_t = out.rearrange("b (t p) d -> b p t d", p=P)

        @block.sync
        def _(sp):
            sp.wait_ge(consts_set, 1)
            for name in ("wq", "wk", "wv"):
                sp.dma_start(raw[name], w[name].rearrange("(t p) n -> p t n", p=P)).then_inc(const_in, 16)
            for tile, row, n, r0 in L.wo_pieces:
                sp.dma_start(raw["wo"][row:row + n, tile, :], w["wo"][r0:r0 + n, :]).then_inc(const_in, 16)
            sp.dma_start(bv_row[:], w["bv"]).then_inc(const_in, 16)
            sp.dma_start(bo_row[:], w["bo"]).then_inc(const_in, 16)
            sp.dma_start(ident[:], ident_d).then_inc(const_in, 16)
            if L.guard:
                sp.dma_start(head_mask[:], w["head_mask"]).then_inc(const_in, 16)
            if L.rms:
                sp.dma_start(bq[:], w["bq"]).then_inc(const_in, 16)
                sp.dma_start(bk[:], w["bk"]).then_inc(const_in, 16)
                sp.dma_start(al_row[:], w["alpha"]).then_inc(const_in, 16)
                sp.dma_start(ga_row[:], w["gamma"]).then_inc(const_in, 16)
            sp.dma_start(x_in[:], x_t[0]).then_inc(x_loaded, 16)
            sp.dma_start(adj_sb[:], adj_t[0]).then_inc(adj_loaded, 16)
            sp.wait_ge(w_lo, len(halves))

            def batch(i, first, last):
                for m in range(M3):
                    for which, (to, done) in enumerate(((L.q_to, q_copied), (L.k_to, k_copied))):
                        sp.wait_ge(qk_lo, i * (2 * M3) + (2 * m + which + 1))
                        if L.tile_heads == H:
                            heads, d = slice(0, H), m * L.tile_dims
                        else:
                            heads, d = slice(m * L.tile_heads, (m + 1) * L.tile_heads), 0
                        for half, s, top in to:
                            sp.dma_start(stack[top + d:top + d + L.tile_dims, s, heads, :].bitcast(F32),
                                         (k_half[:, half] if which else q_half[:, m % q_places, half]).bitcast(F32)
                                         ).then_inc(done, 16)
                if not first:
                    sp.wait_ge(y_ready, i * QT)
                    sp.dma_start(out_t[i - 1], y[:]).then_inc(y_stored, 16)
                sp.wait_ge(x_loaded, i * 16 + 16)
                if not first:
                    sp.wait_ge(y_stored, i * 16)
                sp.dma_start(y[:], x_in[:]).then_inc(x_kept, 16)
                if not last:
                    sp.wait_ge(bank_full, i * R + M3)
                    sp.wait_ge(x_kept, i * 16 + 16)
                    sp.dma_start(x_in[:], x_t[i + 1]).then_inc(x_loaded, 16)
                    sp.wait_ge(s_ready, i * (QT * H) + QT * H)
                    sp.dma_start(adj_sb[:], adj_t[i + 1]).then_inc(adj_loaded, 16)

            batch(0, True, False)
            with sp.Fori(1, B - 1) as i:
                batch(i, False, False)
            batch(B - 1, False, True)
            sp.wait_ge(y_ready, B * QT)
            sp.dma_start(out_t[B - 1], y[:]).then_inc(y_stored, 16)
            sp.wait_ge(y_stored, B * 16)

        @block.gpsimd
        def _(pool):
            pool.memset(ctx_f[:], 0.0).then_inc(consts_set, 1)
            pool.memset(v_hl[:].bitcast(F32), 0.0).then_inc(consts_set, 1)
            pool.memset(minus_half[:], -0.5).then_inc(consts_set, 1)
            if not L.rms:
                pool.memset(bq[:], 0.0).then_inc(consts_set, 1)
                pool.memset(bk[:], 0.0).then_inc(consts_set, 1)
            pool.wait_ge(consts_set, 3 if L.rms else 5)
            def pow_of(i):
                pool.wait_ge(spread_made, i + 1)
                pool.tensor_tensor(out=rstd[:], in0=spread[:], in1=minus_half[:], op=ALU.pow).then_inc(rstd_ready, 1)

            def batch(i, first):
                if not first:
                    pow_of(i - 1)
                for h in range(H):
                    for u in range(2):
                        pool.wait_ge(inv_ready, i * (2 * H) + (2 * h + u + 1))
                        if L.guard:
                            pool.wait_ge(keep_ready, i * (2 * H) + (2 * h + u + 1))
                        pool.sem_inc(norm_begun, 1)
                        for t in (2 * u, 2 * u + 1):
                            place = probs[:, (QT * h + t) % PR]
                            pool.tensor_scalar(out=place, in0=place,
                                               scalar1=row_inv[:, h % 2, t:t + 1],
                                               scalar2=row_keep[:, h % 2, t:t + 1] if L.guard else 1.0,
                                               op0=ALU.mult, op1=ALU.mult).then_inc(p_norm, 1)
                    if h == H // 2:
                        pool.wait_ge(x_kept, i * 16 + 16)
                        for t in range(QT):
                            pool.tensor_tensor(out=y[:, t], in0=y[:, t], in1=bo_row[:], op=ALU.add).then_inc(y_bias, 1)

            batch(0, True)
            with pool.Fori(1, B) as i:
                batch(i, False)
            pow_of(B - 1)

        def split_by_act(act):
            act.wait_ge(const_in, 16 * n_const)
            for name, hi, lo in halves:
                act.activation(hi[:], raw[name], ACT.Copy, scale=q_scale if name == "wq" else 1.0).then_inc(w_hi, 1)

        @block.scalar
        def _(act):
            split_by_act(act)
            if L.rms:
                act.activation(bq[:], bq[:], ACT.Copy, scale=q_scale).then_inc(bias_set, 1)
                act.wait_ge(bias_set, 1)
            with act.Fori(0, B) as i:
                for d in range(M3):
                    act.wait_ge(bank_full, i * R + (XT + d + 1))
                    act.activation(at_h[:, d], ring[:, (XT + d) % RING], ACT.Copy).then_inc(xt_hi, 1)
                for m in range(M3):
                    for which, (bias, to, done) in enumerate(((bq, L.q_to, q_copied), (bk, L.k_to, k_copied))):
                        n = QK + 2 * m + which
                        act.wait_ge(bank_full, i * R + (n + 1))
                        places = 1 if which else q_places
                        if m >= places:
                            act.wait_ge(done, i * (M3 * n_copies[which]) + (m - places + 1) * n_copies[which])
                        if L.guard and not which and m >= places:
                            act.wait_ge(score_sums, i * M3 + (m - places + 1))
                        act.activation(k_half[:, 0] if which else q_half[:, m % q_places, 0], ring[:, n % RING], ACT.Identity,
                                       bias=bias[:, m:m + 1]).then_inc(qk_hi, 1)
                for t in range(QT):
                    act.wait_ge(v_sum, i * QT + (t + 1))
                    act.activation(v_his[t], by_head(v_f[:, t % 2]), ACT.Copy).then_inc(v_hi, 1)
                if L.guard:
                    act.wait_ge(adj_loaded, i * 16 + 16)
                    for t in range(QT):
                        act.activation(probs[:, t], adj_sb[:, t], ACT.Copy,
                                       accum_out=adj_sum[:, t:t + 1]).then_inc(adj_summed, 1)

                def exp_of(h, t):
                    k = QT * h + t
                    act.wait_ge(s_ready, i * (QT * H) + (k + 1))
                    if k >= PR:
                        act.wait_ge(pt_full, i * (2 * H) + ((k - PR) // 2 + 1))
                    act.activation(probs[:, k % PR], neg_s[:, k % NR], ACT.Exp, scale=-1.0,
                                   bias=neg_max[:, h % 2, t:t + 1],
                                   accum_out=row_sum[:, h % 2, t:t + 1]).then_inc(p_exp, 1)

                def pt_half(h, u):
                    act.wait_ge(pt_full, i * (2 * H) + (2 * h + u + 1))
                    if h:
                        act.wait_ge(pv_full, i * (2 * H) + (2 * h + u - 1))
                    act.activation(pt_h[:, :, u * HALF * P:(u + 1) * HALF * P], pt_ps[:, u], ACT.Copy).then_inc(pt_hi, 1)

                def ctx_tile(c):
                    act.wait_ge(ctx_done, i * H + (c + 1) * L.per_tile)
                    act.activation(at_h[:, c], ctx_f[:, c], ACT.Copy).then_inc(ctx_hi, 1)

                for s in range(H + 2):
                    if s < H:
                        exp_of(s, 0)
                        exp_of(s, 1)
                    if 1 <= s <= H:
                        pt_half(s - 1, 0)
                    if s < H:
                        exp_of(s, 2)
                    if s >= 2:
                        act.wait_ge(pv_full, i * (2 * H) + 2 * (s - 1))
                        if L.v_halves_added:
                            act.activation(ctx_lo[:], pv_ps[L.lo_at:L.lo_at + dh], ACT.Copy).then_inc(ctx_part, 1)
                        else:
                            act.activation(ctx_f[slice(*L.ctx_rows(s - 2)), (s - 2) // L.per_tile], pv_ps[0:dh],
                                           ACT.Copy).then_inc(ctx_done, 1)
                    if 1 <= s <= H:
                        pt_half(s - 1, 1)
                    if s < H:
                        exp_of(s, 3)
                    if s >= 3 and (s - 2) % L.per_tile == 0:
                        ctx_tile((s - 2) // L.per_tile - 1)
                ctx_tile(NT - 1)
                if L.rms:
                    for t in range(QT):
                        act.wait_ge(y_res, i * QT + (QT + t + 1))
                        act.activation(probs[:, t, 0:D], y[:, t], ACT.Square,
                                       accum_out=mean_var[:, t, 1:2]).then_inc(y_stat, 1)

        @block.vector
        def _(dve):
            for k, (name, hi, lo) in enumerate(halves):
                dve.wait_ge(w_hi, k + 1)
                dve.scalar_tensor_tensor(out=lo[:], in0=raw[name], scalar=q_scale if name == "wq" else 1.0,
                                         in1=hi[:], op0=ALU.mult, op1=ALU.subtract).then_inc(w_lo, 1)
            dve.wait_ge(w_lo, 4)
            dve.sem_inc(y_res, QT)

            def finish(i):
                if L.rms:
                    dve.wait_ge(y_stat, i * QT + QT)
                    dve.tensor_scalar(out=spread[:], in0=mean_var[:, :, 1], scalar1=1.0 / D, scalar2=RMS_EPS,
                                      op0=ALU.mult, op1=ALU.add).then_inc(spread_made, 1)
                    dve.wait_ge(rstd_ready, i + 1)
                    for t in range(QT):
                        dve.scalar_tensor_tensor(out=y[:, t], in0=y[:, t], scalar=rstd[:, t:t + 1], in1=al_row[:],
                                                 op0=ALU.mult, op1=ALU.mult).then_inc(y_scaled, 1)
                    for t in range(QT):
                        dve.wait_ge(y_scaled, i * QT + (t + 1))
                        dve.tensor_tensor(out=y[:, t], in0=y[:, t], in1=ga_row[:], op=ALU.add).then_inc(y_ready, 1)
                else:
                    for t in range(QT):
                        dve.wait_ge(y_res, i * QT + (QT + t + 1))
                        dve.bn_stats(stat[:, t], y[:, t]).then_inc(y_stat, 1)
                    for t in range(QT):
                        dve.wait_ge(y_stat, i * QT + (t + 1))
                        dve.sem_inc(sum_begun, 1)
                        dve.bn_aggr(mean_var[:, t], stat[:, t]).then_inc(y_scaled, 1)
                    dve.wait_ge(y_scaled, i * QT + QT)
                    dve.tensor_scalar(out=spread[:], in0=mean_var[:, :, 1], scalar1=LN_EPS, scalar2=None,
                                      op0=ALU.add).then_inc(spread_made, 1)
                    dve.wait_ge(rstd_ready, i + 1)
                    for t in range(QT):
                        dve.tensor_scalar(out=y[:, t], in0=y[:, t], scalar1=mean_var[:, t, 0:1],
                                          scalar2=rstd[:, t:t + 1], op0=ALU.subtract, op1=ALU.mult).then_inc(y_ready, 1)

            def batch(i, first):
                for d in range(M3):
                    dve.wait_ge(xt_hi, i * M3 + (d + 1))
                    dve.tensor_tensor(out=at_l[:, d], in0=ring[:, (XT + d) % RING], in1=at_h[:, d],
                                      op=ALU.subtract).then_inc(xt_lo, 1)
                for m in range(M3):
                    for which, (bias, to, done) in enumerate(((bq, L.q_to, q_copied), (bk, L.k_to, k_copied))):
                        n = QK + 2 * m + which
                        dve.wait_ge(qk_hi, i * (2 * M3) + (2 * m + which + 1))
                        if L.guard and which:
                            dve.tensor_reduce(out=k_sum[:, m:m + 1], in_=ring[:, n % RING], axis=AX.X,
                                              op=ALU.add).then_inc(k_summed, 1)
                        half = k_half if which else q_half[:, m % q_places]
                        dve.scalar_tensor_tensor(out=half[:, 1], in0=ring[:, n % RING],
                                                 scalar=bias[:, m:m + 1], in1=half[:, 0],
                                                 op0=ALU.add, op1=ALU.subtract).then_inc(qk_lo, 1)
                        if L.guard and which:
                            dve.wait_ge(k_summed, i * M3 + (m + 1))
                            dve.tensor_scalar(out=k_sum_h[:, m], in0=head_mask[:], scalar1=k_sum[:, m:m + 1],
                                              scalar2=None, op0=ALU.mult).then_inc(k_sum_hi, 1)
                            dve.wait_ge(k_sum_hi, i * M3 + (m + 1))
                            dve.scalar_tensor_tensor(out=k_sum_l[:, m], in0=head_mask[:], scalar=k_sum[:, m:m + 1],
                                                     in1=k_sum_h[:, m], op0=ALU.mult,
                                                     op1=ALU.subtract).then_inc(k_sum_split, 1)
                for t in range(QT + 1):
                    if t < QT:
                        n = VV + t
                        dve.wait_ge(bank_full, i * R + (n + 1))
                        if t >= 2:
                            dve.wait_ge(v_lo, i * QT + (t - 1))
                        dve.tensor_tensor(out=v_f[:, t % 2], in0=ring[:, n % RING, 0:D], in1=bv_row[:],
                                          op=ALU.add).then_inc(v_sum, 1)
                    if t:
                        dve.wait_ge(v_hi, i * QT + t)
                        dve.tensor_tensor(out=v_los[t - 1], in0=by_head(v_f[:, (t - 1) % 2]),
                                          in1=v_his[t - 1], op=ALU.subtract).then_inc(v_lo, 1)

                if L.guard:
                    dve.wait_ge(score_sums, i * M3 + M3)
                    for t in range(QT):
                        dve.wait_ge(adj_summed, i * QT + (t + 1))
                        dve.tensor_scalar(out=sum_nonzero[:, t], in0=pv_ps[:, t * H:(t + 1) * H],
                                          scalar1=adj_sum[:, t:t + 1], scalar2=0.0, op0=ALU.add,
                                          op1=ALU.not_equal).then_inc(sums_tested, 1)
                if not first:
                    finish(i - 1)

                def sum_scores(h, t):
                    k = QT * h + t
                    n = SS + k
                    dve.wait_ge(bank_full, i * R + (n + 1))
                    if k == 0:
                        dve.wait_ge(adj_loaded, i * 16 + 16)
                    if k >= NR:
                        dve.wait_ge(p_exp, i * (QT * H) + (k - NR + 1))
                    if L.guard and h >= 2:
                        dve.wait_ge(keep_ready, i * (2 * H) + (2 * (h - 2) + t // 2 + 1))
                    dve.sem_inc(sum_begun, 1)
                    dve.tensor_tensor_reduce(out=neg_s[:, k % NR], in0=ring[:, n % RING], in1=adj_sb[:, t],
                                             scale=-L.adj_factor, scalar=3.0e38, op0=ALU.add, op1=ALU.min,
                                             accum_out=neg_max[:, h % 2, t:t + 1]).then_inc(s_ready, 1)

                def inverses(h, u):
                    two = slice(2 * u, 2 * u + 2)
                    dve.wait_ge(p_exp, i * (QT * H) + (QT * h + 2 * u + 2))
                    if L.guard:
                        if h == 0 and u == 0:
                            dve.wait_ge(sums_tested, i * QT + QT)
                        dve.scalar_tensor_tensor(out=row_keep[:, h % 2, two], in0=neg_max[:, h % 2, two], scalar=0.0,
                                                 in1=sum_nonzero[:, two, h], op0=ALU.not_equal,
                                                 op1=ALU.max).then_inc(keep_ready, 1)
                    dve.reciprocal(row_inv[:, h % 2, two], row_sum[:, h % 2, two]).then_inc(inv_ready, 1)

                def pt_half(h, u):
                    cols = slice(u * HALF * P, (u + 1) * HALF * P)
                    dve.wait_ge(pt_hi, i * (2 * H) + (2 * h + u + 1))
                    dve.tensor_tensor(out=pt_l[:, :, cols], in0=pt_ps[:, u], in1=pt_h[:, :, cols],
                                      op=ALU.subtract).then_inc(pt_lo, 1)

                def ctx_tile(c):
                    dve.wait_ge(ctx_hi, i * NT + (c + 1))
                    dve.tensor_tensor(out=at_l[:, c], in0=ctx_f[:, c], in1=at_h[:, c],
                                      op=ALU.subtract).then_inc(ctx_lo_done, 1)

                for t in range(QT):
                    sum_scores(0, t)
                for s in range(H + 2):
                    if 1 <= s <= H:
                        inverses(s - 1, 1)
                    if s + 1 < H:
                        sum_scores(s + 1, 0)
                    if s + 1 < H:
                        sum_scores(s + 1, 1)
                    if 1 <= s <= H:
                        pt_half(s - 1, 0)
                    if s < H:
                        inverses(s, 0)
                    if s >= 2 and L.v_halves_added:
                        g = s - 2
                        dve.wait_ge(ctx_part, i * H + (g + 1))
                        dve.tensor_tensor(out=ctx_f[slice(*L.ctx_rows(g)), g // L.per_tile], in0=pv_ps[0:dh],
                                          in1=ctx_lo[:], op=ALU.add).then_inc(ctx_done, 1)
                    if s + 1 < H:
                        sum_scores(s + 1, 2)
                    if 1 <= s <= H:
                        pt_half(s - 1, 1)
                    if s + 1 < H:
                        sum_scores(s + 1, 3)
                    if s >= 3 and (s - 2) % L.per_tile == 0:
                        ctx_tile((s - 2) // L.per_tile - 1)
                ctx_tile(NT - 1)
                dve.wait_ge(y_bias, i * QT + QT)
                for t in range(QT):
                    n = OO + t
                    dve.wait_ge(bank_full, i * R + (n + 1))
                    dve.tensor_tensor(out=y[:, t], in0=ring[:, n % RING, 0:D], in1=y[:, t],
                                      op=ALU.add).then_inc(y_res, 1)

            batch(0, True)
            with dve.Fori(1, B) as i:
                batch(i, False)
            finish(B - 1)

        @block.tensor
        def _(pe):
            pe.wait_ge(w_lo, 4)
            pe.wait_ge(consts_set, 3 if L.rms else 5)
            with pe.Fori(0, B) as i:
                def claim(n):
                    m = prior(n)
                    if m < 0:
                        pe.wait_ge(y_res, i * QT + (m + R - OO + 1))
                    else:
                        start, done, each = [u for u in ((XT, xt_lo, M3), (QK, qk_lo, 2 * M3), (VV, v_sum, QT),
                                                         (SS, s_ready, QT * H), (OO, y_res, QT)) if u[0] <= m][-1]
                        pe.wait_ge(done, i * each + (m - start + 1 + (QT if done is y_res else 0)))
                    return ring[:, n % RING]

                pe.wait_ge(x_loaded, i * 16 + 16)
                for d in range(M3):
                    bank = claim(XT + d)
                    for t in range(QT):
                        last = pe.transpose(bank[:, t * P:(t + 1) * P], x_in[:, t, d * P:(d + 1) * P], ident[:])
                    last.then_inc(bank_full, 1)

                def sum_of_scores(m):
                    pe.wait_ge(k_sum_split, i * M3 + (m + 1))
                    for t in range(QT):
                        at = t * H + m * L.tile_heads
                        to, toks = pv_ps[:, at:at + L.tile_heads], slice(t * P, (t + 1) * P)
                        for k, (half, sums) in enumerate(((0, k_sum_h), (0, k_sum_l), (1, k_sum_h), (1, k_sum_l))):
                            last = pe.matmul(to, q_half[:, m % q_places, half, toks], sums[:, m],
                                             start=(k == 0), stop=(k == 3))
                    last.then_inc(score_sums, 1)

                for m in range(M3):
                    for which, (w_h_, w_l_) in enumerate(((wq_h, wq_l), (wk_h, wk_l))):
                        n = QK + 2 * m + which
                        bank = claim(n)
                        for d in range(M3):
                            if m == 0 and which == 0:
                                pe.wait_ge(xt_lo, i * M3 + (d + 1))
                            cols = slice(m * P, (m + 1) * P)
                            pe.matmul(bank, w_h_[:, d, cols], at_h[:, d], start=(d == 0), stop=False)
                            pe.matmul(bank, w_h_[:, d, cols], at_l[:, d], start=False, stop=False)
                            last = pe.matmul(bank, w_l_[:, d, cols], at_h[:, d], start=False, stop=(d == M3 - 1))
                        last.then_inc(bank_full, 1)
                    if L.guard and m:
                        sum_of_scores(m - 1)
                for t in range(QT):
                    bank = claim(VV + t)[:, 0:D]
                    toks = slice(t * P, (t + 1) * P)
                    for d in range(M3):
                        pe.matmul(bank, at_h[:, d, toks], wv_h[:, d], start=(d == 0), stop=False)
                        pe.matmul(bank, at_h[:, d, toks], wv_l[:, d], start=False, stop=False)
                        last = pe.matmul(bank, at_l[:, d, toks], wv_h[:, d], start=False, stop=(d == M3 - 1))
                    last.then_inc(bank_full, 1)
                    if L.guard and t == 0:
                        sum_of_scores(M3 - 1)

                def score(h, t):
                    bank = claim(SS + QT * h + t)
                    for s in range(1, L.stacks):
                        last = pe.matmul(bank, stack[0:L.rows, 0, h, t * P:(t + 1) * P],
                                         stack[0:L.rows, s, h, :], start=(s == 1), stop=(s == L.stacks - 1))
                    last.then_inc(bank_full, 1)

                def weigh(h, u):
                    pe.wait_ge(pt_lo, i * (2 * H) + (2 * h + u + 1))
                    if L.guard and h == 0 and u == 0:
                        pe.wait_ge(sums_tested, i * QT + QT)
                    if h and u == 0:
                        pe.wait_ge(ctx_done, i * H + h)
                    cols = slice(u * HALF * P, (u + 1) * HALF * P)
                    for t in range(QT):
                        if L.v_halves_added:
                            to, hi = pv_ps[0:2 * L.lo_at, cols], v_hl[:, t, h, :]
                        else:
                            to, hi = pv_ps[0:dh, cols], v_hl[:, t, h, 0:dh]
                        pe.matmul(to, hi, pt_h[:, t, cols], start=(t == 0), stop=False)
                        if not L.v_halves_added:
                            pe.matmul(to, v_hl[:, t, h, dh:2 * dh], pt_h[:, t, cols], start=False, stop=False)
                        last = pe.matmul(to, hi, pt_l[:, t, cols], start=False, stop=(t == QT - 1))
                    last.then_inc(pv_full, 1)

                def transposed(h, u):
                    pe.wait_ge(p_norm, i * (QT * H) + (QT * h + 2 * u + 2))
                    if h:
                        pe.wait_ge(pt_lo, i * (2 * H) + (2 * h + u - 1))
                    for c in range(QT):
                        for k in range(HALF):
                            last = pe.transpose(pt_ps[:, u, c, k * P:(k + 1) * P],
                                                probs[:, (QT * h + HALF * u + k) % PR, c * P:(c + 1) * P], ident[:])
                    last.then_inc(pt_full, 1)

                pe.wait_ge(q_copied, i * (M3 * n_copies[0]) + M3 * n_copies[0])
                pe.wait_ge(k_copied, i * (M3 * n_copies[1]) + M3 * n_copies[1])
                for t in range(QT):
                    score(0, t)
                pe.wait_ge(v_lo, i * QT + QT)
                score(1, 0)
                for s in range(H + 2):
                    if s + 1 < H:
                        score(s + 1, 1)
                    if 1 <= s <= H:
                        transposed(s - 1, 0)
                    if s >= 2:
                        weigh(s - 2, 1)
                    if s + 1 < H:
                        score(s + 1, 2)
                    if 1 <= s <= H:
                        transposed(s - 1, 1)
                    if s + 1 < H:
                        score(s + 1, 3)
                    if 1 <= s <= H:
                        weigh(s - 1, 0)
                    if s + 2 < H:
                        score(s + 2, 0)
                pe.wait_ge(ctx_lo_done, i * NT + NT)
                for t in range(QT):
                    bank = claim(OO + t)[:, 0:D]
                    toks = slice(t * P, (t + 1) * P)
                    for c in range(NT):
                        pe.matmul(bank, at_h[:, c, toks], wo_h[:, c], start=(c == 0), stop=False)
                        pe.matmul(bank, at_h[:, c, toks], wo_l[:, c], start=False, stop=False)
                        last = pe.matmul(bank, at_l[:, c, toks], wo_h[:, c], start=False, stop=(c == NT - 1))
                    last.then_inc(bank_full, 1)


def feed_forward_layer(nc, a, x, w, ident_d, out):
    B, N, D = a.shape
    FT = w["w1"].shape[1] // P
    M3, QT = D // P, N // P
    RING = 4
    LAG = 2
    R = M3 + FT

    with ExitStack() as ctx:
        def sb(name, shape, dt=F32):
            return ctx.enter_context(nc.sbuf_tensor(f"ff_{name}", shape, dt))

        def sem(name):
            return ctx.enter_context(nc.semaphore(f"ff_{name}"))

        w1_raw, w2_raw = sb("w1_raw", [P, M3, FT * P]), sb("w2_raw", [P, FT, D])
        w1_h, w1_l = sb("w1_h", [P, M3, FT * P], F32R), sb("w1_l", [P, M3, FT * P], F32R)
        w2_h, w2_l = sb("w2_h", [P, FT, D], F32R), sb("w2_l", [P, FT, D], F32R)
        b1, b1_half = sb("b1", [P, FT]), sb("b1_half", [P, FT])
        b2_row, al_row, ga_row = (sb(n, [P, D]) for n in ("b2_row", "al_row", "ga_row"))
        ident, minus_half = sb("ident", [P, P]), sb("minus_half", [P, QT])
        a_in, a_res, x_res, y = (sb(n, [P, QT, D]) for n in ("a_in", "a_res", "x_res", "y"))
        at_h, at_l = sb("at_h", [P, M3, N], F32R), sb("at_l", [P, M3, N], F32R)
        tanh, lin, act_f = (sb(n, [P, 2, N]) for n in ("tanh", "lin", "act_f"))
        hid_h, hid_l = sb("hid_h", [P, 3, N], F32R), sb("hid_l", [P, 3, N], F32R)
        junk, total = sb("junk", [P, QT, D]), sb("total", [P, QT, D])
        stat, mean_var = sb("stat", [P, QT, 6]), sb("mean_var", [P, QT, 2])
        squares, spread, rstd = sb("squares", [P, QT]), sb("spread", [P, 2, QT]), sb("rstd", [P, 2, QT])

        ring = ctx.enter_context(nc.psum_tensor("ff_ring", [P, RING, N], F32))
        sums = ctx.enter_context(nc.psum_tensor("ff_sums", [P, QT, N], F32))

        const_in, consts_set, w_hi, w_lo = (sem(n) for n in ("const_in", "consts_set", "w_hi", "w_lo"))
        a_loaded, a_kept, x_loaded, x_gamma = (sem(n) for n in ("a_loaded", "a_kept", "x_loaded", "x_gamma"))
        bank_full, xt_hi, xt_lo, h_lin, h_mul, h_hi, h_lo = (
            sem(n) for n in ("bank_full", "xt_hi", "xt_lo", "h_lin", "h_mul", "h_hi", "h_lo"))
        down_done, sums_full = sem("down_done"), sem("sums_full")
        y_sum, y_res, y_square, y_scaled, y_mixed, y_stat, y_aggr, spread_made, rstd_ready, y_ready, y_stored = (
            sem(n) for n in ("y_sum", "y_res", "y_square", "y_scaled", "y_mixed", "y_stat", "y_aggr",
                             "spread_made", "rstd_ready", "y_ready", "y_stored"))
        block = ctx.enter_context(nc.Block())
        a_t, x_t, out_t = (v.rearrange("b (t p) d -> b p t d", p=P) for v in (a, x, out))

        @block.sync
        def _(sp):
            sp.dma_start(w1_raw[:], w["w1"].rearrange("(t p) n -> p t n", p=P)).then_inc(const_in, 16)
            sp.dma_start(w2_raw[:], w["w2"].rearrange("(t p) n -> p t n", p=P)).then_inc(const_in, 16)
            for to, what in ((b1, "b1"), (b2_row, "b2"), (al_row, "alpha"), (ga_row, "gamma")):
                sp.dma_start(to[:], w[what]).then_inc(const_in, 16)
            sp.dma_start(ident[:], ident_d).then_inc(const_in, 16)
            sp.dma_start(a_in[:], a_t[0]).then_inc(a_loaded, 16)

            def batch(i, first, last):
                if not first:
                    sp.wait_ge(y_res, i * QT)
                sp.wait_ge(a_loaded, i * 16 + 16)
                sp.dma_start(a_res[:], a_in[:]).then_inc(a_kept, 16)
                if not last:
                    sp.wait_ge(bank_full, i * R + M3)
                    sp.wait_ge(a_kept, i * 16 + 16)
                    sp.dma_start(a_in[:], a_t[i + 1]).then_inc(a_loaded, 16)
                if not first:
                    sp.wait_ge(y_mixed, i * QT)
                sp.dma_start(x_res[:], x_t[i]).then_inc(x_loaded, 16)
                if not first:
                    sp.wait_ge(y_ready, i * QT)
                    sp.dma_start(out_t[i - 1], y[:]).then_inc(y_stored, 16)

            batch(0, True, False)
            with sp.Fori(1, B - 1) as i:
                batch(i, False, False)
            batch(B - 1, False, True)
            sp.wait_ge(y_ready, B * QT)
            sp.dma_start(out_t[B - 1], y[:]).then_inc(y_stored, 16)
            sp.wait_ge(y_stored, B * 16)

        @block.gpsimd
        def _(pool):
            pool.memset(minus_half[:], -0.5).then_inc(consts_set, 1)
            pool.wait_ge(consts_set, 1)
            pool.wait_ge(const_in, 16 * 7)

            def add_gamma(i):
                pool.wait_ge(x_loaded, i * 16 + 16)
                for t in range(QT):
                    pool.tensor_tensor(out=x_res[:, t], in0=x_res[:, t], in1=ga_row[:], op=ALU.add).then_inc(x_gamma, 1)

            def pow_of(i, k):
                pool.wait_ge(spread_made, i * 2 + (k + 1))
                pool.tensor_tensor(out=rstd[:, k], in0=spread[:, k], in1=minus_half[:],
                                   op=ALU.pow).then_inc(rstd_ready, 1)

            add_gamma(0)
            with pool.Fori(1, B) as i:
                pow_of(i - 1, 0)
                add_gamma(i)
                pow_of(i - 1, 1)
            pow_of(B - 1, 0)
            pow_of(B - 1, 1)

        @block.scalar
        def _(act):
            act.wait_ge(const_in, 16 * 7)
            act.activation(w1_h[:], w1_raw[:], ACT.Copy).then_inc(w_hi, 1)
            act.activation(w2_h[:], w2_raw[:], ACT.Copy, scale=0.5).then_inc(w_hi, 1)
            act.activation(b1_half[:], b1[:], ACT.Copy, scale=0.5).then_inc(w_hi, 1)
            act.wait_ge(w_hi, 3)

            def x_transposed(i):
                for d in range(M3):
                    act.wait_ge(bank_full, i * R + (d + 1))
                    act.activation(at_h[:, d], ring[:, d % RING], ACT.Copy).then_inc(xt_hi, 1)

            def squares_of(i):
                for t in range(QT):
                    act.wait_ge(y_res, i * QT + (t + 1))
                    act.activation(junk[:, t], y[:, t], ACT.Square, accum_out=squares[:, t:t + 1]).then_inc(y_square, 1)

            def batch(i, first, last):
                for f in range(FT + 1):
                    if f < FT:
                        n = M3 + f
                        act.wait_ge(bank_full, i * R + (n + 1))
                        act.activation(tanh[:, f % 2], ring[:, n % RING], ACT.Tanh, scale=0.5, bias=b1_half[:, f:f + 1])
                        act.activation(lin[:, f % 2], ring[:, n % RING], ACT.Identity,
                                       bias=b1[:, f:f + 1]).then_inc(h_lin, 1)
                    if f:
                        g = f - 1
                        act.wait_ge(h_mul, i * FT + (g + 1))
                        if g >= 3:
                            act.wait_ge(down_done, i * (FT - 1) + (g - 2))
                        elif not first and g < 2:
                            act.wait_ge(down_done, i * (FT - 1) + (g - 1))
                        elif not first:
                            act.wait_ge(sums_full, i * QT)
                        act.activation(hid_h[:, g % 3], act_f[:, g % 2], ACT.Copy).then_inc(h_hi, 1)
                    if f == 3 and not first:
                        squares_of(i - 1)
                if not last:
                    x_transposed(i + 1)

            x_transposed(0)
            batch(0, True, False)
            with act.Fori(1, B - 1) as i:
                batch(i, False, False)
            batch(B - 1, False, True)
            squares_of(B - 1)

        @block.vector
        def _(dve):
            dve.wait_ge(w_hi, 1)
            dve.tensor_tensor(out=w1_l[:], in0=w1_raw[:], in1=w1_h[:], op=ALU.subtract).then_inc(w_lo, 1)
            dve.wait_ge(w_hi, 2)
            dve.scalar_tensor_tensor(out=w2_l[:], in0=w2_raw[:], scalar=0.5, in1=w2_h[:],
                                     op0=ALU.mult, op1=ALU.subtract).then_inc(w_lo, 1)
            dve.sem_inc(y_sum, QT)

            def x_transposed(i):
                for d in range(M3):
                    dve.wait_ge(xt_hi, i * M3 + (d + 1))
                    dve.tensor_tensor(out=at_l[:, d], in0=ring[:, d % RING], in1=at_h[:, d],
                                      op=ALU.subtract).then_inc(xt_lo, 1)

            def finish_part(i, f, first):
                if f in (1, 2):
                    if f == 1:
                        dve.wait_ge(a_kept, i * 16 + 16)
                        if not first:
                            dve.wait_ge(y_stored, i * 16)
                    for t in (2 * f - 2, 2 * f - 1):
                        dve.wait_ge(y_sum, i * QT + (QT + t + 1))
                        dve.tensor_tensor(out=y[:, t], in0=total[:, t], in1=a_res[:, t], op=ALU.add).then_inc(y_res, 1)
                if f == 4:
                    dve.wait_ge(y_square, i * QT + QT)
                    dve.tensor_scalar(out=spread[:, 0], in0=squares[:], scalar1=1.0 / D, scalar2=RMS_EPS,
                                      op0=ALU.mult, op1=ALU.add).then_inc(spread_made, 1)
                if f in (5, 6):
                    dve.wait_ge(rstd_ready, i * 2 + 1)
                    for t in (2 * f - 10, 2 * f - 9):
                        dve.scalar_tensor_tensor(out=y[:, t], in0=y[:, t], scalar=rstd[:, 0, t:t + 1], in1=al_row[:],
                                                 op0=ALU.mult, op1=ALU.mult).then_inc(y_scaled, 1)
                if f in (7, 8):
                    for t in (2 * f - 14, 2 * f - 13):
                        dve.wait_ge(x_gamma, i * QT + (t + 1))
                        dve.wait_ge(y_scaled, i * QT + (t + 1))
                        dve.tensor_tensor(out=y[:, t], in0=y[:, t], in1=x_res[:, t], op=ALU.add).then_inc(y_mixed, 1)
                if f in (9, 10):
                    for t in (2 * f - 18, 2 * f - 17):
                        dve.wait_ge(y_mixed, i * QT + (t + 1))
                        dve.bn_stats(stat[:, t], y[:, t]).then_inc(y_stat, 1)
                if f == 11:
                    for t in range(QT):
                        dve.wait_ge(w_lo, 2)
                        dve.wait_ge(y_stat, i * QT + (t + 1))
                        dve.bn_aggr(mean_var[:, t], stat[:, t]).then_inc(y_aggr, 1)
                    dve.wait_ge(y_aggr, i * QT + QT)
                    dve.tensor_scalar(out=spread[:, 1], in0=mean_var[:, :, 1], scalar1=LN_EPS, scalar2=None,
                                      op0=ALU.add).then_inc(spread_made, 1)
                if f == FT:
                    dve.wait_ge(rstd_ready, i * 2 + 2)
                    for t in range(QT):
                        dve.tensor_scalar(out=y[:, t], in0=y[:, t], scalar1=mean_var[:, t, 0:1],
                                          scalar2=rstd[:, 1, t:t + 1], op0=ALU.subtract, op1=ALU.mult).then_inc(y_ready, 1)

            def batch(i, first, second, last):
                for f in range(FT + 1):
                    if f < FT:
                        dve.wait_ge(h_lin, i * FT + (f + 1))
                        if f >= 2 or not first:
                            dve.wait_ge(h_lo, i * FT + (f - 1))
                        dve.scalar_tensor_tensor(out=act_f[:, f % 2], in0=tanh[:, f % 2], scalar=1.0, in1=lin[:, f % 2],
                                                 op0=ALU.add, op1=ALU.mult).then_inc(h_mul, 1)
                    if f:
                        g = f - 1
                        dve.wait_ge(h_hi, i * FT + (g + 1))
                        dve.tensor_tensor(out=hid_l[:, g % 3], in0=act_f[:, g % 2], in1=hid_h[:, g % 3],
                                          op=ALU.subtract).then_inc(h_lo, 1)
                    if not first and f < FT:
                        finish_part(i - 1, f, second)
                if not last:
                    x_transposed(i + 1)
                if not first:
                    finish_part(i - 1, FT, second)
                for t in range(QT):
                    if not first:
                        dve.wait_ge(y_res, i * QT - (QT - 1) + t)
                    dve.wait_ge(sums_full, i * QT + (t + 1))
                    dve.tensor_tensor(out=total[:, t], in0=sums[:, t, 0:D], in1=b2_row[:], op=ALU.add).then_inc(y_sum, 1)

            x_transposed(0)
            batch(0, True, False, False)
            batch(1, False, True, False)
            with dve.Fori(2, B - 1) as i:
                batch(i, False, False, False)
            batch(B - 1, False, False, True)
            for f in range(FT + 1):
                finish_part(B - 1, f, False)

        @block.tensor
        def _(pe):
            pe.wait_ge(w_lo, 2)
            pe.wait_ge(const_in, 16 * 7)

            def x_transposed(i, first):
                pe.wait_ge(a_loaded, i * 16 + 16)
                for d in range(M3):
                    if not first:
                        pe.wait_ge(h_lin, i * FT - (M3 - 1 - d))
                    for t in range(QT):
                        last = pe.transpose(ring[:, d, t * P:(t + 1) * P], a_in[:, t, d * P:(d + 1) * P], ident[:])
                    last.then_inc(bank_full, 1)

            def batch(i, last_batch):
                def up(f):
                    n = M3 + f
                    if n < RING + M3 and n >= RING:
                        pe.wait_ge(xt_lo, i * M3 + (n - RING + 1))
                    elif n >= RING:
                        pe.wait_ge(h_lin, i * FT + (n - RING - M3 + 1))
                    bank, cols = ring[:, n % RING], slice(f * P, (f + 1) * P)
                    for d in range(M3):
                        if f == 0:
                            pe.wait_ge(xt_lo, i * M3 + (d + 1))
                        pe.matmul(bank, w1_h[:, d, cols], at_h[:, d], start=(d == 0), stop=False)
                        pe.matmul(bank, w1_h[:, d, cols], at_l[:, d], start=False, stop=False)
                        last = pe.matmul(bank, w1_l[:, d, cols], at_h[:, d], start=False, stop=(d == M3 - 1))
                    last.then_inc(bank_full, 1)

                def down(f):
                    pe.wait_ge(h_lo, i * FT + (f + 1))
                    for t in range(QT):
                        if f == 0:
                            pe.wait_ge(y_sum, i * QT + (t + 1))
                        toks = slice(t * P, (t + 1) * P)
                        pe.matmul(sums[:, t, 0:D], hid_h[:, f % 3, toks], w2_h[:, f], start=(f == 0), stop=False)
                        pe.matmul(sums[:, t, 0:D], hid_h[:, f % 3, toks], w2_l[:, f], start=False, stop=False)
                        last = pe.matmul(sums[:, t, 0:D], hid_l[:, f % 3, toks], w2_h[:, f],
                                         start=False, stop=(f == FT - 1))
                        if f == FT - 1:
                            last.then_inc(sums_full, 1)
                    if f < FT - 1:
                        last.then_inc(down_done, 1)

                for f in range(FT + LAG):
                    if f < FT:
                        up(f)
                    if f >= LAG:
                        down(f - LAG)
                    if f == FT and not last_batch:
                        x_transposed(i + 1, False)

            x_transposed(0, True)
            with pe.Fori(0, B - 1) as i:
                batch(i, False)
            batch(B - 1, True)


def build(nc, a, out, B, N, D):
    x1 = nc.dram_tensor("attended_dram", (B, N, D), F32, kind="Internal").ap()
    x2 = nc.dram_tensor("layer_0_dram", (B, N, D), F32, kind="Internal").ap()
    attention_layer(nc, Layer("a0", 8, 48, 2, 1.0, True, False), a["x"], a["adj"],
                    {k: a[f"L0_gnn_{n}"] for k, n in (("wq", "wq"), ("wk", "wk"), ("wv", "wv"), ("wo", "wo"), ("bq", "bq"),
                                                      ("bk", "bk"), ("bv", "bv"), ("bo", "bo"), ("alpha", "alpha1"),
                                                      ("gamma", "gamma1"))}, a["ident"], x1)
    feed_forward_layer(nc, x1, a["x"], {k: a[f"L0_gnn_{n}"] for k, n in (("w1", "w1"), ("w2", "w2"), ("b1", "b1"),
                                                                         ("b2", "b2"), ("alpha", "alpha2"),
                                                                         ("gamma", "gamma2"))}, a["ident"], x2)
    attention_layer(nc, Layer("a1", 12, 32, 1, 2.0, False, True), x2, a["adj"],
                    dict({k: a[f"L1_gnn_{n}"] for k, n in (("wq", "Wq"), ("wk", "Wk"), ("wv", "Wv"), ("wo", "Wo"),
                                                           ("bv", "bv"), ("bo", "bo"))}, head_mask=a["head_mask"]),
                    a["ident"], out)


COLUMNS = ("L0_gnn_bq", "L0_gnn_bk", "L0_gnn_b1")
BY_DIMENSION = ("L0_gnn_wq", "L0_gnn_bq", "L0_gnn_wk", "L0_gnn_bk")
BY_DIMENSION_1 = ("L1_gnn_Wq", "L1_gnn_Wk")
ROWS = ("L0_gnn_bv", "L0_gnn_bo", "L0_gnn_b2", "L0_gnn_alpha1", "L0_gnn_gamma1", "L0_gnn_alpha2",
        "L0_gnn_gamma2", "L1_gnn_bv", "L1_gnn_bo")
TRANSPOSED = ("L1_gnn_Wq", "L1_gnn_Wk", "L1_gnn_Wv", "L1_gnn_Wo")


def kernel(**inputs):
    import numpy as _np
    import concourse.bacc as _bacc
    from concourse import mybir as _mybir
    from concourse.bass_utils import run_bass_kernel_spmd as _run

    nc = _bacc.Bacc("TRN2", target_bir_lowering=False, num_devices=1)
    inputs = dict(inputs, ident=_np.eye(P, dtype=_np.float32),
                  head_mask=_np.tile(_np.eye(4, dtype=_np.float32), (32, 1)))
    arrays, args = {}, {}
    for name, v in inputs.items():
        v = _np.asarray(v)
        if name in ROWS:
            v = _np.broadcast_to(v, (P, v.shape[0]))
        elif name in TRANSPOSED:
            v = v.T
        if name in BY_DIMENSION:
            v = _np.moveaxis(v.reshape(*v.shape[:-1], 8, 3, 16), -3, -1).reshape(v.shape)
        if name in BY_DIMENSION_1:
            v = v.reshape(-1, 3, 4, 32).swapaxes(-2, -1).reshape(v.shape)
        if name in COLUMNS:
            v = v.reshape(-1, P).T
        v = _np.ascontiguousarray(v)
        arrays[f"in_{name}_dram"] = v
        args[name] = nc.dram_tensor(f"in_{name}_dram", v.shape, _mybir.dt.from_np(v.dtype), kind="ExternalInput").ap()
    B, N, D = inputs["x"].shape
    out = nc.dram_tensor("out_0_dram", (B, N, D), _mybir.dt.float32, kind="ExternalOutput").ap()
    build(nc, args, out, B, N, D)
    r = _run(nc, [arrays], core_ids=[0])
    return r.results[0]["out_0_dram"]
```

```python
from contextlib import ExitStack

import concourse.bass as bass
from concourse import mybir

P = 128
ALU = mybir.AluOpType
ACT = mybir.ActivationFunctionType
AX = mybir.AxisListType
F32 = mybir.dt.float32
F32R = mybir.dt.float32r
RMS_EPS = 1e-6
LN_EPS = 1e-5


class Layer:

    def __init__(self, name, heads, dim, passes, adj_factor, rms, guard):
        self.name, self.H, self.dh, self.passes = name, heads, dim, passes
        self.adj_factor, self.rms, self.guard = adj_factor, rms, guard
        D = heads * dim
        self.rows = 2 * dim if passes == 2 else 4 * dim
        self.lo_at = 64 if dim > 32 else 32
        self.per_tile = 2 if dim > 32 else 4
        self.row_step = P // self.per_tile
        self.NT = heads // self.per_tile
        self.v_halves_added = passes == 2
        self.wo_pieces = [(h // self.per_tile, (h % self.per_tile) * self.row_step, dim, h * dim) for h in range(heads)]
        self.tile_dims = P // heads if passes == 2 else dim
        self.tile_heads = P // self.tile_dims
        if passes == 2:
            self.q_to = [(0, 0, 0), (1, 0, dim)]
            self.k_to = [(0, 1, 0), (1, 1, dim), (1, 2, 0), (0, 2, dim)]
        else:
            self.q_to = [(0, 0, 0), (0, 0, dim), (1, 0, 2 * dim), (1, 0, 3 * dim)]
            self.k_to = [(0, 1, 0), (1, 1, dim), (0, 1, 2 * dim), (1, 1, 3 * dim)]
        self.stacks = 1 + len({s for _, s, _ in self.k_to})

    def ctx_rows(self, head):
        row = (head % self.per_tile) * self.row_step
        return row, row + self.dh


def attention_layer(nc, L, x, adj, w, ident_d, out):
    B, N, D = x.shape
    H, dh, NT, M3, QT = L.H, L.dh, L.NT, D // P, N // P
    SCALE = (float(dh) ** -0.5) if L.rms else (float(D) ** -0.5)
    q_scale = SCALE / L.adj_factor
    HALF = QT // 2

    SS, XT = 0, QT * H
    QK = XT + M3
    VV = QK + 2 * M3
    ZZ = VV + QT
    OO = ZZ + (1 if L.guard else 0)
    R = OO + QT
    AHEAD = OO - XT
    RING = 3

    def uses(i, n, last=False):
        if isinstance(i, int) and i < 0:
            return QT + (n - XT + 1)
        return i * R + (R - XT) + n + 1 - (AHEAD if last and n >= XT else 0)

    def prior(n, last):
        here = [m for m in range(n) if m % RING == n % RING and not (last and XT <= m < OO)]
        return here[-1] if here else max(m for m in range(R) if m % RING == n % RING) - R

    n_copies = [16 * len(to) for to in (L.q_to, L.k_to)]

    PR = 6
    FINISH_STEPS = 5
    POW_STEP = 0 if L.rms else 2
    NR = 5

    with ExitStack() as ctx:
        def sb(name, shape, dt=F32):
            return ctx.enter_context(nc.sbuf_tensor(f"{L.name}_{name}", shape, dt))

        def sem(name):
            return ctx.enter_context(nc.semaphore(f"{L.name}_{name}"))

        wq_h, wk_h, wv_h = (sb(n, [P, M3, D], F32R) for n in ("wq_h", "wk_h", "wv_h"))
        wq_l, wk_l, wv_l = (sb(n, [P, M3, D], F32R) for n in ("wq_l", "wk_l", "wv_l"))
        wo_h, wo_l = sb("wo_h", [P, NT, D], F32R), sb("wo_l", [P, NT, D], F32R)
        bq, bk = sb("bq", [P, M3]), sb("bk", [P, M3])
        bo_row = sb("bo_row", [P, D])
        bv_row = None if L.rms else sb("bv_row", [P, D])
        bv_col = sb("bv_col", [dh, H]) if L.rms else None
        al_row, ga_row = (sb("al_row", [P, D]), sb("ga_row", [P, D])) if L.rms else (None, None)
        ident = sb("ident", [P, P])
        minus_half = sb("minus_half", [P, QT])
        adj_sb = sb("adj", [P, QT, N])
        x_in = sb("x_in", [P, QT, D])
        at_h, at_l = sb("at_h", [P, M3, N], F32R), sb("at_l", [P, M3, N], F32R)
        ct_h, ct_l = sb("ct_h", [P, NT, N], F32R), sb("ct_l", [P, NT, N], F32R)
        ctx_f = sb("ctx_f", [P, 2, N])
        q_places = 3 if L.guard else 1
        q_half = sb("q_half", [P, q_places, 2, N], F32R)
        k_half = sb("k_half", [P, 2, N], F32R)
        if L.guard:
            k_sum, head_mask = sb("k_sum", [P, M3]), sb("head_mask", [P, L.tile_heads])
            k_sums = sb("k_sums", [P, M3, 2, L.tile_heads], F32R)
            adj_sum, score_sum = sb("adj_sum", [P, QT]), sb("score_sum", [P, QT, H])
            sum_nonzero = sb("sum_nonzero", [P, QT, H])
        stack = sb("stack", [P, L.stacks, H, N], F32R)
        v_f = None if L.rms else sb("v_f", [P, 2, D])
        v_hl = sb("v_hl", [P, QT, H, L.lo_at + dh], F32R)
        probs = sb("probs", [P, PR, N])
        neg_s = sb("neg_s", [P, NR, N])
        neg_max, row_sum, row_inv, row_keep = (sb(n, [P, 2, QT]) for n in ("neg_max", "row_sum", "row_inv", "row_keep"))
        pt_h, pt_l = sb("pt_h", [P, QT, N], F32R), sb("pt_l", [P, QT, N], F32R)
        y = sb("y", [P, QT, D])
        stat = sb("stat", [P, QT, 6])
        mean_var = sb("mean_var", [P, QT, 2])
        spread, rstd = sb("spread", [P, QT]), sb("rstd", [P, QT])

        ring = ctx.enter_context(nc.psum_tensor(f"{L.name}_ring", [P, RING, N], F32))
        pt_ps = ctx.enter_context(nc.psum_tensor(f"{L.name}_pt_ps", [P, 2, QT, HALF * P], F32))
        pv_ps = ctx.enter_context(nc.psum_tensor(f"{L.name}_pv_ps", [P, N], F32))

        first_in, const_in, consts_set, w_hi, w_lo, bias_set = (
            sem(n) for n in ("first_in", "const_in", "consts_set", "w_hi", "w_lo", "bias_set"))
        norm_begun, sum_begun = sem("norm_begun"), sem("sum_begun")
        x_loaded, adj_loaded, x_kept = sem("x_loaded"), sem("adj_loaded"), sem("x_kept")
        bank_full = sem("bank_full")
        xt_hi, xt_lo = sem("xt_hi"), sem("xt_lo")
        qk_hi, qk_lo = sem("qk_hi"), sem("qk_lo")
        q_copied, k_copied = sem("q_copied"), sem("k_copied")
        v_sum, v_hi, v_lo = sem("v_sum"), sem("v_hi"), sem("v_lo")
        k_summed, k_sum_hi, k_sum_split, scores_summed, adj_summed, sums_tested = (
            sem(n) for n in ("k_summed", "k_sum_hi", "k_sum_split", "scores_summed", "adj_summed", "sums_tested"))
        s_ready, p_exp, keep_ready, inv_ready, p_norm = (sem(n) for n in ("s_ready", "p_exp", "keep_ready", "inv_ready", "p_norm"))
        pt_full, pt_hi, pt_lo = sem("pt_full"), sem("pt_hi"), sem("pt_lo")
        pv_full, ctx_part, ctx_done = sem("pv_full"), sem("ctx_part"), sem("ctx_done")
        ctx_hi, ctx_lo_done = sem("ctx_hi"), sem("ctx_lo_done")
        y_bias, y_res, y_stat, spread_made, rstd_ready, y_scaled, y_ready, y_stored = (
            sem(n) for n in ("y_bias", "y_res", "y_stat", "spread_made", "rstd_ready", "y_scaled", "y_ready", "y_stored"))
        block = ctx.enter_context(nc.Block())

        def staged(ap, tiles):
            return ap.rearrange("p a b -> p (a b)")[:, 0:tiles * D].rearrange("p (a b) -> p a b", a=tiles)

        raw = {"wq": staged(probs[:, 0:3], M3), "wk": staged(probs[:, 3:6], M3), "wv": staged(y[:], M3),
               "wo": staged(neg_s[:], NT)}
        by_head = lambda ap: ap.rearrange("p (h d) -> p h d", h=H)
        v_his = [v_hl[:, t, :, 0:dh] for t in range(QT)]
        v_los = [v_hl[:, t, :, L.lo_at:L.lo_at + dh] for t in range(QT)]
        n_first = 3 + (2 if L.rms else 0) + (1 if L.guard else 0)
        n_const = 3 + len(L.wo_pieces) + (2 if L.rms else 0)
        halves = [("wq", wq_h, wq_l), ("wk", wk_h, wk_l), ("wv", wv_h, wv_l), ("wo", wo_h, wo_l)]
        x_t = x.rearrange("b (t p) d -> b p t d", p=P)
        adj_t = adj.rearrange("b (t p) n -> b p t n", p=P)
        out_t = out.rearrange("b (t p) d -> b p t d", p=P)

        @block.sync
        def _(sp):
            sp.dma_start(ident[:], ident_d).then_inc(first_in, 16)
            sp.dma_start(x_in[:], x_t[0]).then_inc(x_loaded, 16)
            for name in ("wq", "wk"):
                sp.dma_start(raw[name], w[name].rearrange("(t p) n -> p t n", p=P)).then_inc(first_in, 16)
            if L.guard:
                sp.dma_start(head_mask[:], w["head_mask"]).then_inc(first_in, 16)
            if L.rms:
                sp.dma_start(bq[:], w["bq"]).then_inc(first_in, 16)
                sp.dma_start(bk[:], w["bk"]).then_inc(first_in, 16)
            sp.dma_start(raw["wv"], w["wv"].rearrange("(t p) n -> p t n", p=P)).then_inc(const_in, 16)
            sp.dma_start(bv_col[:] if L.rms else bv_row[:], w["bv"]).then_inc(const_in, 16)
            sp.wait_ge(consts_set, 1)
            for tile, row, n, r0 in L.wo_pieces:
                sp.dma_start(raw["wo"][row:row + n, tile, :], w["wo"][r0:r0 + n, :]).then_inc(const_in, 16)
            sp.dma_start(bo_row[:], w["bo"]).then_inc(const_in, 16)
            if L.rms:
                sp.dma_start(al_row[:], w["alpha"]).then_inc(const_in, 16)
                sp.dma_start(ga_row[:], w["gamma"]).then_inc(const_in, 16)
            sp.dma_start(adj_sb[:], adj_t[0]).then_inc(adj_loaded, 16)

            def to_stacks(i):
                for m in range(M3):
                    for which, (to, done) in enumerate(((L.q_to, q_copied), (L.k_to, k_copied))):
                        sp.wait_ge(qk_lo, i * (2 * M3) + (2 * m + which + 1))
                        if L.tile_heads == H:
                            heads, d = slice(0, H), m * L.tile_dims
                        else:
                            heads, d = slice(m * L.tile_heads, (m + 1) * L.tile_heads), 0
                        for half, s, top in to:
                            sp.dma_start(stack[top + d:top + d + L.tile_dims, s, heads, :].bitcast(F32),
                                         (k_half[:, half] if which else q_half[:, m % q_places, half]).bitcast(F32)
                                         ).then_inc(done, 16)

            def batch(i, first, last):
                if not first:
                    sp.wait_ge(y_ready, i * QT)
                    sp.dma_start(out_t[i - 1], y[:]).then_inc(y_stored, 16)
                    sp.wait_ge(y_stored, i * 16)
                sp.dma_start(y[:], x_in[:]).then_inc(x_kept, 16)
                if not last:
                    sp.wait_ge(x_kept, i * 16 + 16)
                    sp.dma_start(x_in[:], x_t[i + 1]).then_inc(x_loaded, 16)
                    sp.wait_ge(s_ready, i * (QT * H) + QT * H)
                    sp.dma_start(adj_sb[:], adj_t[i + 1]).then_inc(adj_loaded, 16)
                    to_stacks(i + 1)

            to_stacks(0)
            sp.wait_ge(w_lo, len(halves))
            batch(0, True, False)
            with sp.Fori(1, B - 1) as i:
                batch(i, False, False)
            batch(B - 1, False, True)
            sp.wait_ge(y_ready, B * QT)
            sp.dma_start(out_t[B - 1], y[:]).then_inc(y_stored, 16)
            sp.wait_ge(y_stored, B * 16)

        @block.gpsimd
        def _(pool):
            pool.memset(neg_s[:], 0.0).then_inc(consts_set, 1)
            pool.memset(ctx_f[:], 0.0).then_inc(consts_set, 1)
            pool.memset(v_hl[:].bitcast(F32), 0.0).then_inc(consts_set, 1)
            pool.memset(minus_half[:], -0.5).then_inc(consts_set, 1)
            if not L.rms:
                pool.memset(bq[:], 0.0).then_inc(consts_set, 1)
                pool.memset(bk[:], 0.0).then_inc(consts_set, 1)
            pool.wait_ge(consts_set, 4 if L.rms else 6)
            pool.wait_ge(const_in, 16 * n_const)
            def pow_of(i):
                pool.wait_ge(spread_made, i + 1)
                pool.tensor_tensor(out=rstd[:], in0=spread[:], in1=minus_half[:], op=ALU.pow).then_inc(rstd_ready, 1)

            def batch(i, first):
                for h in range(H):
                    for u in range(2):
                        pool.wait_ge(inv_ready, i * (2 * H) + (2 * h + u + 1))
                        if L.guard:
                            pool.wait_ge(keep_ready, i * (2 * H) + (2 * h + u + 1))
                        pool.sem_inc(norm_begun, 1)
                        for t in (2 * u, 2 * u + 1):
                            place = probs[:, (QT * h + t) % PR]
                            pool.tensor_scalar(out=place, in0=place,
                                               scalar1=row_inv[:, h % 2, t:t + 1],
                                               scalar2=row_keep[:, h % 2, t:t + 1] if L.guard else 1.0,
                                               op0=ALU.mult, op1=ALU.mult).then_inc(p_norm, 1)
                        if not first and h == POW_STEP and u == 0:
                            pow_of(i - 1)
                    if h == H - 2:
                        pool.wait_ge(x_kept, i * 16 + 16)
                        for t in range(QT):
                            pool.tensor_tensor(out=y[:, t], in0=y[:, t], in1=bo_row[:], op=ALU.add).then_inc(y_bias, 1)

            batch(0, True)
            with pool.Fori(1, B) as i:
                batch(i, False)
            pow_of(B - 1)

        @block.scalar
        def _(act):
            def split(which):
                for name, hi, lo in which:
                    act.activation(hi[:], raw[name], ACT.Copy, scale=q_scale if name == "wq" else 1.0).then_inc(w_hi, 1)

            act.wait_ge(first_in, 16 * n_first)
            act.wait_ge(consts_set, 4 if L.rms else 6)
            split(halves[:2])
            if L.rms:
                act.activation(bq[:], bq[:], ACT.Copy, scale=q_scale).then_inc(bias_set, 1)
                act.wait_ge(bias_set, 1)

            def x_tiles(i):
                for d in range(M3):
                    act.wait_ge(bank_full, uses(i - 1, XT + d))
                    act.activation(at_h[:, d], ring[:, (XT + d) % RING], ACT.Copy).then_inc(xt_hi, 1)

            def qk_tiles(i, m):
                for which, (bias, to, done) in enumerate(((bq, L.q_to, q_copied), (bk, L.k_to, k_copied))):
                    n = QK + 2 * m + which
                    act.wait_ge(bank_full, uses(i - 1, n))
                    places = 1 if which else q_places
                    if m >= places:
                        act.wait_ge(done, i * (M3 * n_copies[which]) + (m - places + 1) * n_copies[which])
                    act.activation(k_half[:, 0] if which else q_half[:, m % q_places, 0], ring[:, n % RING],
                                   ACT.Identity, bias=bias[:, m:m + 1]).then_inc(qk_hi, 1)

            def v_tiles(i):
                for t in range(QT):
                    if L.rms:
                        act.wait_ge(bank_full, uses(i - 1, VV + t))
                        act.activation(v_his[t], by_head(ring[:, (VV + t) % RING, 0:D]), ACT.Copy).then_inc(v_hi, 1)
                    else:
                        act.wait_ge(v_sum, i * QT + (t + 1))
                        act.activation(v_his[t], by_head(v_f[:, t % 2]), ACT.Copy).then_inc(v_hi, 1)
                if L.guard:
                    act.wait_ge(adj_loaded, i * 16 + 16)
                    for t in range(QT):
                        act.activation(probs[:, t], adj_sb[:, t], ACT.Copy,
                                       accum_out=adj_sum[:, t:t + 1]).then_inc(adj_summed, 1)

            def batch(i, last):
                def exp_of(h, t):
                    k = QT * h + t
                    act.wait_ge(s_ready, i * (QT * H) + (k + 1))
                    if k >= PR:
                        act.wait_ge(pt_full, i * (2 * H) + ((k - PR) // 2 + 1))
                    act.activation(probs[:, k % PR], neg_s[:, k % NR], ACT.Exp, scale=-1.0,
                                   bias=neg_max[:, h % 2, t:t + 1],
                                   accum_out=row_sum[:, h % 2, t:t + 1]).then_inc(p_exp, 1)

                def pt_half(h, u):
                    act.wait_ge(pt_full, i * (2 * H) + (2 * h + u + 1))
                    if h:
                        act.wait_ge(pv_full, i * (2 * H) + (2 * h + u - 1))
                    act.activation(pt_h[:, :, u * HALF * P:(u + 1) * HALF * P], pt_ps[:, u], ACT.Copy).then_inc(pt_hi, 1)

                def ctx_tile(c):
                    act.wait_ge(ctx_done, i * H + (c + 1) * L.per_tile)
                    act.activation(ct_h[:, c], ctx_f[:, c % 2], ACT.Copy).then_inc(ctx_hi, 1)

                for s in range(H + 2):
                    if s == H - 1 and not last:
                        x_tiles(i + 1)
                    if s < H:
                        exp_of(s, 0)
                        exp_of(s, 1)
                    if 1 <= s <= H:
                        pt_half(s - 1, 0)
                    if s < H:
                        exp_of(s, 2)
                    if s >= 2:
                        act.wait_ge(pv_full, i * (2 * H) + 2 * (s - 1))
                        c, in_tile = divmod(s - 2, L.per_tile)
                        if in_tile == 0 and c != 1:
                            act.wait_ge(ctx_lo_done, i * NT + (NT + max(c - 1, 0)))
                        part = L.lo_at if L.v_halves_added else 0
                        act.activation(ctx_f[slice(*L.ctx_rows(s - 2)), c % 2], pv_ps[part:part + dh],
                                       ACT.Copy).then_inc(ctx_part if L.v_halves_added else ctx_done, 1)
                    if 1 <= s <= H:
                        pt_half(s - 1, 1)
                    if s < H:
                        exp_of(s, 3)
                    if s >= 3 and (s - 2) % L.per_tile == 0:
                        ctx_tile((s - 2) // L.per_tile - 1)
                    if s >= H - 1 and not last:
                        qk_tiles(i + 1, s - (H - 1))
                ctx_tile(NT - 1)
                if not last:
                    v_tiles(i + 1)
                if L.rms:
                    for t in range(QT):
                        act.wait_ge(y_res, i * QT + (QT + t + 1))
                        act.activation(probs[:, t, 0:D], y[:, t], ACT.Square,
                                       accum_out=mean_var[:, t, 1:2]).then_inc(y_stat, 1)
                    act.wait_ge(y_stat, i * QT + QT)

            x_tiles(0)
            for m in range(M3):
                qk_tiles(0, m)
            act.wait_ge(const_in, 16 * n_const)
            split(halves[2:])
            v_tiles(0)
            with act.Fori(0, B - 1) as i:
                batch(i, False)
            batch(B - 1, True)

        @block.vector
        def _(dve):
            def split(of):
                for k in of:
                    name, hi, lo = halves[k]
                    dve.wait_ge(w_hi, k + 1)
                    dve.scalar_tensor_tensor(out=lo[:], in0=raw[name], scalar=q_scale if name == "wq" else 1.0,
                                             in1=hi[:], op0=ALU.mult, op1=ALU.subtract).then_inc(w_lo, 1)

            split((0, 1))
            dve.sem_inc(y_res, QT)
            dve.sem_inc(ctx_lo_done, NT)

            def finish_part(i, s):
                if L.rms:
                    if s == 0:
                        dve.wait_ge(y_stat, i * QT + QT)
                        dve.tensor_scalar(out=spread[:], in0=mean_var[:, :, 1], scalar1=1.0 / D, scalar2=RMS_EPS,
                                          op0=ALU.mult, op1=ALU.add).then_inc(spread_made, 1)
                    if s in (1, 2):
                        dve.wait_ge(rstd_ready, i + 1)
                        for t in (2 * s - 2, 2 * s - 1):
                            dve.scalar_tensor_tensor(out=y[:, t], in0=y[:, t], scalar=rstd[:, t:t + 1], in1=al_row[:],
                                                     op0=ALU.mult, op1=ALU.mult).then_inc(y_scaled, 1)
                    if s in (3, 4):
                        for t in (2 * s - 6, 2 * s - 5):
                            dve.wait_ge(y_scaled, i * QT + (t + 1))
                            dve.tensor_tensor(out=y[:, t], in0=y[:, t], in1=ga_row[:], op=ALU.add).then_inc(y_ready, 1)
                else:
                    if s in (0, 1):
                        for t in (2 * s, 2 * s + 1):
                            dve.wait_ge(y_res, i * QT + (QT + t + 1))
                            dve.bn_stats(stat[:, t], y[:, t]).then_inc(y_stat, 1)
                    if s == 2:
                        for t in range(QT):
                            dve.wait_ge(y_stat, i * QT + (t + 1))
                            dve.sem_inc(sum_begun, 1)
                            dve.bn_aggr(mean_var[:, t], stat[:, t]).then_inc(y_scaled, 1)
                        dve.wait_ge(y_scaled, i * QT + QT)
                        dve.tensor_scalar(out=spread[:], in0=mean_var[:, :, 1], scalar1=LN_EPS, scalar2=None,
                                          op0=ALU.add).then_inc(spread_made, 1)
                    if s in (3, 4):
                        dve.wait_ge(rstd_ready, i + 1)
                        for t in (2 * s - 6, 2 * s - 5):
                            dve.tensor_scalar(out=y[:, t], in0=y[:, t], scalar1=mean_var[:, t, 0:1],
                                              scalar2=rstd[:, t:t + 1], op0=ALU.subtract, op1=ALU.mult).then_inc(y_ready, 1)

            def x_tiles(i):
                for d in range(M3):
                    dve.wait_ge(xt_hi, i * M3 + (d + 1))
                    dve.tensor_tensor(out=at_l[:, d], in0=ring[:, (XT + d) % RING], in1=at_h[:, d],
                                      op=ALU.subtract).then_inc(xt_lo, 1)

            def qk_tiles(i, m):
                for which, bias in enumerate((bq, bk)):
                    n = QK + 2 * m + which
                    dve.wait_ge(qk_hi, i * (2 * M3) + (2 * m + which + 1))
                    if L.guard and which:
                        dve.tensor_reduce(out=k_sum[:, m:m + 1], in_=ring[:, n % RING], axis=AX.X,
                                          op=ALU.add).then_inc(k_summed, 1)
                    half = k_half if which else q_half[:, m % q_places]
                    dve.scalar_tensor_tensor(out=half[:, 1], in0=ring[:, n % RING],
                                             scalar=bias[:, m:m + 1], in1=half[:, 0],
                                             op0=ALU.add, op1=ALU.subtract).then_inc(qk_lo, 1)
                    if L.guard and which:
                        dve.wait_ge(k_summed, i * M3 + (m + 1))
                        dve.tensor_scalar(out=k_sums[:, m, 0], in0=head_mask[:], scalar1=k_sum[:, m:m + 1],
                                          scalar2=None, op0=ALU.mult).then_inc(k_sum_hi, 1)
                        dve.wait_ge(k_sum_hi, i * M3 + (m + 1))
                        dve.scalar_tensor_tensor(out=k_sums[:, m, 1], in0=head_mask[:], scalar=k_sum[:, m:m + 1],
                                                 in1=k_sums[:, m, 0], op0=ALU.mult,
                                                 op1=ALU.subtract).then_inc(k_sum_split, 1)

            def v_tiles(i, first):
                if L.rms:
                    for t in range(QT):
                        dve.wait_ge(v_hi, i * QT + (t + 1))
                        dve.tensor_tensor(out=v_los[t], in0=by_head(ring[:, (VV + t) % RING, 0:D]),
                                          in1=v_his[t], op=ALU.subtract).then_inc(v_lo, 1)
                    return
                for t in range(QT + 1):
                    if t < QT:
                        n = VV + t
                        dve.wait_ge(bank_full, uses(i - 1, n))
                        if t >= 2 or not first:
                            dve.wait_ge(v_lo, i * QT + (t - 1))
                        dve.tensor_tensor(out=v_f[:, t % 2], in0=ring[:, n % RING, 0:D], in1=bv_row[:],
                                          op=ALU.add).then_inc(v_sum, 1)
                    if t:
                        dve.wait_ge(v_hi, i * QT + t)
                        dve.tensor_tensor(out=v_los[t - 1], in0=by_head(v_f[:, (t - 1) % 2]),
                                          in1=v_his[t - 1], op=ALU.subtract).then_inc(v_lo, 1)
                dve.wait_ge(bank_full, uses(i - 1, ZZ))
                if not first:
                    dve.wait_ge(keep_ready, i * (2 * H))
                sums = ring[:, ZZ % RING, 0:QT * M3 * 2 * L.tile_heads].rearrange(
                    "p (t m k h) -> p t m k h", t=QT, m=M3, k=2)
                for t in range(QT):
                    dve.wait_ge(adj_summed, i * QT + (t + 1))
                    by_tile = score_sum[:, t].rearrange("p (m h) -> p m h", m=M3)
                    dve.tensor_scalar(out=by_tile, in0=sums[:, t, :, 0], scalar1=adj_sum[:, t:t + 1], scalar2=None,
                                      op0=ALU.add).then_inc(scores_summed, 1)
                    dve.wait_ge(scores_summed, i * (2 * QT) + (2 * t + 1))
                    dve.tensor_tensor(out=by_tile, in0=sums[:, t, :, 1], in1=by_tile, op=ALU.add).then_inc(scores_summed, 1)
                dve.wait_ge(scores_summed, i * (2 * QT) + 2 * QT)
                dve.tensor_scalar(out=sum_nonzero[:], in0=score_sum[:], scalar1=0.0, scalar2=None,
                                  op0=ALU.not_equal).then_inc(sums_tested, 1)

            def batch(i, first, last):
                def sum_scores(h, t):
                    k = QT * h + t
                    n = SS + k
                    dve.wait_ge(bank_full, uses(i, n))
                    if k == 0:
                        dve.wait_ge(adj_loaded, i * 16 + 16)
                    if k >= NR:
                        dve.wait_ge(p_exp, i * (QT * H) + (k - NR + 1))
                    if L.guard and h >= 2:
                        dve.wait_ge(keep_ready, i * (2 * H) + (2 * (h - 2) + t // 2 + 1))
                    dve.sem_inc(sum_begun, 1)
                    dve.tensor_tensor_reduce(out=neg_s[:, k % NR], in0=ring[:, n % RING], in1=adj_sb[:, t],
                                             scale=-L.adj_factor, scalar=3.0e38, op0=ALU.add, op1=ALU.min,
                                             accum_out=neg_max[:, h % 2, t:t + 1]).then_inc(s_ready, 1)

                def inverses(h, u):
                    two = slice(2 * u, 2 * u + 2)
                    dve.wait_ge(p_exp, i * (QT * H) + (QT * h + 2 * u + 2))
                    if L.guard:
                        if h == 0 and u == 0:
                            dve.wait_ge(sums_tested, i + 1)
                        dve.scalar_tensor_tensor(out=row_keep[:, h % 2, two], in0=neg_max[:, h % 2, two], scalar=0.0,
                                                 in1=sum_nonzero[:, two, h], op0=ALU.not_equal,
                                                 op1=ALU.max).then_inc(keep_ready, 1)
                    dve.reciprocal(row_inv[:, h % 2, two], row_sum[:, h % 2, two]).then_inc(inv_ready, 1)

                def pt_half(h, u):
                    cols = slice(u * HALF * P, (u + 1) * HALF * P)
                    dve.wait_ge(pt_hi, i * (2 * H) + (2 * h + u + 1))
                    dve.tensor_tensor(out=pt_l[:, :, cols], in0=pt_ps[:, u], in1=pt_h[:, :, cols],
                                      op=ALU.subtract).then_inc(pt_lo, 1)

                def ctx_tile(c):
                    dve.wait_ge(ctx_hi, i * NT + (c + 1))
                    dve.tensor_tensor(out=ct_l[:, c], in0=ctx_f[:, c % 2], in1=ct_h[:, c],
                                      op=ALU.subtract).then_inc(ctx_lo_done, 1)

                for t in range(QT):
                    sum_scores(0, t)
                for s in range(H + 2):
                    if s == H - 1 and not last:
                        x_tiles(i + 1)
                    if 1 <= s <= H:
                        inverses(s - 1, 1)
                    if s + 1 < H:
                        sum_scores(s + 1, 0)
                    if s + 1 < H:
                        sum_scores(s + 1, 1)
                    if 1 <= s <= H:
                        pt_half(s - 1, 0)
                    if s < H:
                        inverses(s, 0)
                    if s >= 2 and L.v_halves_added:
                        g = s - 2
                        dve.wait_ge(ctx_part, i * H + (g + 1))
                        rows = ctx_f[slice(*L.ctx_rows(g)), g // L.per_tile % 2]
                        dve.scalar_tensor_tensor(out=rows, in0=pv_ps[0:dh], scalar=bv_col[:, g:g + 1], in1=rows,
                                                 op0=ALU.add, op1=ALU.add).then_inc(ctx_done, 1)
                    if s + 1 < H:
                        sum_scores(s + 1, 2)
                    if 1 <= s <= H:
                        pt_half(s - 1, 1)
                    if s + 1 < H:
                        sum_scores(s + 1, 3)
                    if s >= 3 and (s - 2) % L.per_tile == 0:
                        ctx_tile((s - 2) // L.per_tile - 1)
                    if not first and s < FINISH_STEPS:
                        finish_part(i - 1, s)
                    if s >= H - 1 and not last:
                        qk_tiles(i + 1, s - (H - 1))
                ctx_tile(NT - 1)
                if not last:
                    v_tiles(i + 1, False)
                dve.wait_ge(y_bias, i * QT + QT)
                for t in range(QT):
                    n = OO + t
                    dve.wait_ge(bank_full, uses(i, n, last))
                    dve.tensor_tensor(out=y[:, t], in0=ring[:, n % RING, 0:D], in1=y[:, t],
                                      op=ALU.add).then_inc(y_res, 1)

            x_tiles(0)
            for m in range(M3):
                qk_tiles(0, m)
            split((2, 3))
            dve.wait_ge(const_in, 16 * n_const)
            dve.wait_ge(w_lo, 4)
            v_tiles(0, True)
            batch(0, True, False)
            with dve.Fori(1, B - 1) as i:
                batch(i, False, False)
            batch(B - 1, False, True)
            for s in range(FINISH_STEPS):
                finish_part(B - 1, s)

        @block.tensor
        def _(pe):
            pe.wait_ge(first_in, 16 * n_first)
            stages = ((SS, s_ready, QT * H, 0), (XT, xt_lo, M3, 1), (QK, qk_lo, 2 * M3, 1),
                      (VV, v_lo if L.rms else v_sum, QT, 1), (ZZ, sums_tested, 1, 1), (OO, y_res, QT, 1))

            def claim(i, n, before=False, last=False):
                m = prior(n, last)
                if before and m < XT:
                    return ring[:, n % RING]
                turn, m = (i, m) if m >= 0 else (i - 1, m + R)
                start, done, each, ahead = [u for u in stages if u[0] <= m][-1]
                pe.wait_ge(done, turn * each + (ahead * each + m - start + 1))
                return ring[:, n % RING]

            def x_tiles(i, before=False):
                pe.wait_ge(x_loaded, i * 16 + 16)
                for d in range(M3):
                    bank = claim(i - 1, XT + d, before)
                    for t in range(QT):
                        last = pe.transpose(bank[:, t * P:(t + 1) * P], x_in[:, t, d * P:(d + 1) * P], ident[:])
                    last.then_inc(bank_full, 1)

            def qk_tiles(i, m, before=False):
                for which, (w_h_, w_l_) in enumerate(((wq_h, wq_l), (wk_h, wk_l))):
                    bank = claim(i - 1, QK + 2 * m + which, before)
                    for d in range(M3):
                        if m == 0 and which == 0:
                            pe.wait_ge(xt_lo, i * M3 + (d + 1))
                        cols = slice(m * P, (m + 1) * P)
                        pe.matmul(bank, w_h_[:, d, cols], at_h[:, d], start=(d == 0), stop=False)
                        pe.matmul(bank, w_h_[:, d, cols], at_l[:, d], start=False, stop=False)
                        last = pe.matmul(bank, w_l_[:, d, cols], at_h[:, d], start=False, stop=(d == M3 - 1))
                    last.then_inc(bank_full, 1)

            def v_tiles(i, before=False):
                for t in range(QT):
                    bank = claim(i - 1, VV + t, before)[:, 0:D]
                    toks = slice(t * P, (t + 1) * P)
                    for d in range(M3):
                        pe.matmul(bank, at_h[:, d, toks], wv_h[:, d], start=(d == 0), stop=False)
                        pe.matmul(bank, at_h[:, d, toks], wv_l[:, d], start=False, stop=False)
                        last = pe.matmul(bank, at_l[:, d, toks], wv_h[:, d], start=False, stop=(d == M3 - 1))
                    last.then_inc(bank_full, 1)
                if L.guard:
                    bank = claim(i - 1, ZZ, before)
                    pe.wait_ge(k_sum_split, i * M3 + M3)
                    for m in range(M3):
                        for t in range(QT):
                            at = (t * M3 + m) * 2 * L.tile_heads
                            to, toks = bank[:, at:at + 2 * L.tile_heads], slice(t * P, (t + 1) * P)
                            for half in range(2):
                                last = pe.matmul(to, q_half[:, m % q_places, half, toks],
                                                 k_sums[:, m].rearrange("p k h -> p (k h)"),
                                                 start=(half == 0), stop=(half == 1))
                    last.then_inc(bank_full, 1)

            def batch(i, last_batch):
                def score(h, t):
                    bank = claim(i, SS + QT * h + t)
                    for s in range(1, L.stacks):
                        last = pe.matmul(bank, stack[0:L.rows, 0, h, t * P:(t + 1) * P],
                                         stack[0:L.rows, s, h, :], start=(s == 1), stop=(s == L.stacks - 1))
                    last.then_inc(bank_full, 1)

                def weigh(h, u):
                    pe.wait_ge(pt_lo, i * (2 * H) + (2 * h + u + 1))
                    if h and u == 0:
                        pe.wait_ge(ctx_done, i * H + h)
                    cols = slice(u * HALF * P, (u + 1) * HALF * P)
                    for t in range(QT):
                        if L.v_halves_added:
                            to, hi = pv_ps[0:L.lo_at + dh, cols], v_hl[:, t, h, :]
                        else:
                            to, hi = pv_ps[0:dh, cols], v_hl[:, t, h, 0:dh]
                        pe.matmul(to, hi, pt_h[:, t, cols], start=(t == 0), stop=False)
                        if not L.v_halves_added:
                            pe.matmul(to, v_hl[:, t, h, dh:2 * dh], pt_h[:, t, cols], start=False, stop=False)
                        last = pe.matmul(to, hi, pt_l[:, t, cols], start=False, stop=(t == QT - 1))
                    last.then_inc(pv_full, 1)

                def transposed(h, u):
                    pe.wait_ge(p_norm, i * (QT * H) + (QT * h + 2 * u + 2))
                    if h:
                        pe.wait_ge(pt_lo, i * (2 * H) + (2 * h + u - 1))
                    for c in range(QT):
                        for k in range(HALF):
                            last = pe.transpose(pt_ps[:, u, c, k * P:(k + 1) * P],
                                                probs[:, (QT * h + HALF * u + k) % PR, c * P:(c + 1) * P], ident[:])
                    last.then_inc(pt_full, 1)

                pe.wait_ge(q_copied, i * (M3 * n_copies[0]) + M3 * n_copies[0])
                pe.wait_ge(k_copied, i * (M3 * n_copies[1]) + M3 * n_copies[1])
                for t in range(QT):
                    score(0, t)
                pe.wait_ge(v_lo, i * QT + QT)
                score(1, 0)
                for s in range(H + 2):
                    if s + 1 < H:
                        score(s + 1, 1)
                    if 1 <= s <= H:
                        transposed(s - 1, 0)
                    if s >= 2:
                        weigh(s - 2, 1)
                    if s + 1 < H:
                        score(s + 1, 2)
                    if 1 <= s <= H:
                        transposed(s - 1, 1)
                    if s >= H - 1 and not last_batch:
                        qk_tiles(i + 1, s - (H - 1))
                    if s + 1 < H:
                        score(s + 1, 3)
                    if 1 <= s <= H:
                        weigh(s - 1, 0)
                    if s + 2 < H:
                        score(s + 2, 0)
                    if s == H - 2 and not last_batch:
                        x_tiles(i + 1)
                if not last_batch:
                    v_tiles(i + 1)
                pe.wait_ge(ctx_lo_done, i * NT + 2 * NT)
                for t in range(QT):
                    bank = claim(i, OO + t, last=last_batch)[:, 0:D]
                    toks = slice(t * P, (t + 1) * P)
                    for c in range(NT):
                        pe.matmul(bank, ct_h[:, c, toks], wo_h[:, c], start=(c == 0), stop=False)
                        pe.matmul(bank, ct_h[:, c, toks], wo_l[:, c], start=False, stop=False)
                        last = pe.matmul(bank, ct_l[:, c, toks], wo_h[:, c], start=False, stop=(c == NT - 1))
                    last.then_inc(bank_full, 1)

            pe.sem_inc(bank_full, QT)
            x_tiles(0, True)
            pe.wait_ge(w_lo, 2)
            for m in range(M3):
                qk_tiles(0, m, True)
            pe.wait_ge(w_lo, 4)
            pe.wait_ge(consts_set, 4 if L.rms else 6)
            v_tiles(0, True)
            pe.wait_ge(v_lo, QT)
            if L.guard:
                pe.wait_ge(sums_tested, 1)
            with pe.Fori(0, B - 1) as i:
                batch(i, False)
            batch(B - 1, True)


def feed_forward_layer(nc, a, x, w, ident_d, out):
    B, N, D = a.shape
    FT = w["w1"].shape[1] // P
    M3, QT = D // P, N // P
    RING = 4
    LAG = 2
    R = M3 + FT

    with ExitStack() as ctx:
        def sb(name, shape, dt=F32):
            return ctx.enter_context(nc.sbuf_tensor(f"ff_{name}", shape, dt))

        def sem(name):
            return ctx.enter_context(nc.semaphore(f"ff_{name}"))

        w1_raw, w2_raw = sb("w1_raw", [P, M3, FT * P]), sb("w2_raw", [P, FT, D])
        w1_h, w1_l = sb("w1_h", [P, M3, FT * P], F32R), sb("w1_l", [P, M3, FT * P], F32R)
        w2_h, w2_l = sb("w2_h", [P, FT, D], F32R), sb("w2_l", [P, FT, D], F32R)
        b1, b1_half = sb("b1", [P, FT]), sb("b1_half", [P, FT])
        b2_row, al_row, ga_row = (sb(n, [P, D]) for n in ("b2_row", "al_row", "ga_row"))
        ident, minus_half = sb("ident", [P, P]), sb("minus_half", [P, QT])
        a_in, a_res, x_res, y = (sb(n, [P, QT, D]) for n in ("a_in", "a_res", "x_res", "y"))
        at_h, at_l = sb("at_h", [P, M3, N], F32R), sb("at_l", [P, M3, N], F32R)
        tanh, lin, act_f = (sb(n, [P, 2, N]) for n in ("tanh", "lin", "act_f"))
        hid_h, hid_l = sb("hid_h", [P, 3, N], F32R), sb("hid_l", [P, 3, N], F32R)
        junk, total = sb("junk", [P, QT, D]), sb("total", [P, QT, D])
        stat, mean_var = sb("stat", [P, QT, 6]), sb("mean_var", [P, QT, 2])
        squares, spread, rstd = sb("squares", [P, QT]), sb("spread", [P, 2, QT]), sb("rstd", [P, 2, QT])

        ring = ctx.enter_context(nc.psum_tensor("ff_ring", [P, RING, N], F32))
        sums = ctx.enter_context(nc.psum_tensor("ff_sums", [P, QT, N], F32))

        first_in, const_in, consts_set, w_hi, w_lo = (
            sem(n) for n in ("first_in", "const_in", "consts_set", "w_hi", "w_lo"))
        a_loaded, a_kept, x_loaded, x_gamma = (sem(n) for n in ("a_loaded", "a_kept", "x_loaded", "x_gamma"))
        bank_full, xt_hi, xt_lo, h_lin, h_mul, h_hi, h_lo = (
            sem(n) for n in ("bank_full", "xt_hi", "xt_lo", "h_lin", "h_mul", "h_hi", "h_lo"))
        down_done, sums_full = sem("down_done"), sem("sums_full")
        y_sum, y_res, y_square, y_scaled, y_mixed, y_stat, y_aggr, spread_made, rstd_ready, y_ready, y_stored = (
            sem(n) for n in ("y_sum", "y_res", "y_square", "y_scaled", "y_mixed", "y_stat", "y_aggr",
                             "spread_made", "rstd_ready", "y_ready", "y_stored"))
        block = ctx.enter_context(nc.Block())
        a_t, x_t, out_t = (v.rearrange("b (t p) d -> b p t d", p=P) for v in (a, x, out))

        @block.sync
        def _(sp):
            sp.dma_start(ident[:], ident_d).then_inc(first_in, 16)
            sp.dma_start(a_in[:], a_t[0]).then_inc(a_loaded, 16)
            sp.dma_start(w1_raw[:], w["w1"].rearrange("(t p) n -> p t n", p=P)).then_inc(first_in, 16)
            sp.dma_start(b1[:], w["b1"]).then_inc(first_in, 16)
            sp.dma_start(w2_raw[:], w["w2"].rearrange("(t p) n -> p t n", p=P)).then_inc(const_in, 16)
            for to, what in ((b2_row, "b2"), (al_row, "alpha"), (ga_row, "gamma")):
                sp.dma_start(to[:], w[what]).then_inc(const_in, 16)

            def batch(i, first, last):
                if not first:
                    sp.wait_ge(y_res, i * QT)
                sp.wait_ge(a_loaded, i * 16 + 16)
                sp.dma_start(a_res[:], a_in[:]).then_inc(a_kept, 16)
                if not last:
                    sp.wait_ge(bank_full, i * R + M3)
                    sp.wait_ge(a_kept, i * 16 + 16)
                    sp.dma_start(a_in[:], a_t[i + 1]).then_inc(a_loaded, 16)
                if not first:
                    sp.wait_ge(y_mixed, i * QT)
                sp.dma_start(x_res[:], x_t[i]).then_inc(x_loaded, 16)
                if not first:
                    sp.wait_ge(y_ready, i * QT)
                    sp.dma_start(out_t[i - 1], y[:]).then_inc(y_stored, 16)

            batch(0, True, False)
            with sp.Fori(1, B - 1) as i:
                batch(i, False, False)
            batch(B - 1, False, True)
            sp.wait_ge(y_ready, B * QT)
            sp.dma_start(out_t[B - 1], y[:]).then_inc(y_stored, 16)
            sp.wait_ge(y_stored, B * 16)

        @block.gpsimd
        def _(pool):
            pool.memset(minus_half[:], -0.5).then_inc(consts_set, 1)
            pool.wait_ge(consts_set, 1)
            pool.wait_ge(const_in, 16 * 4)

            def add_gamma(i):
                pool.wait_ge(x_loaded, i * 16 + 16)
                for t in range(QT):
                    pool.tensor_tensor(out=x_res[:, t], in0=x_res[:, t], in1=ga_row[:], op=ALU.add).then_inc(x_gamma, 1)

            def pow_of(i, k):
                pool.wait_ge(spread_made, i * 2 + (k + 1))
                pool.tensor_tensor(out=rstd[:, k], in0=spread[:, k], in1=minus_half[:],
                                   op=ALU.pow).then_inc(rstd_ready, 1)

            add_gamma(0)
            with pool.Fori(1, B) as i:
                pow_of(i - 1, 0)
                add_gamma(i)
                pow_of(i - 1, 1)
            pow_of(B - 1, 0)
            pow_of(B - 1, 1)

        @block.scalar
        def _(act):
            act.wait_ge(first_in, 16 * 3)
            act.activation(w1_h[:], w1_raw[:], ACT.Copy).then_inc(w_hi, 1)
            act.activation(b1_half[:], b1[:], ACT.Copy, scale=0.5).then_inc(w_hi, 1)

            def x_transposed(i):
                for d in range(M3):
                    act.wait_ge(bank_full, i * R + (d + 1))
                    act.activation(at_h[:, d], ring[:, d % RING], ACT.Copy).then_inc(xt_hi, 1)

            def squares_of(i):
                for t in range(QT):
                    act.wait_ge(y_res, i * QT + (t + 1))
                    act.activation(junk[:, t], y[:, t], ACT.Square, accum_out=squares[:, t:t + 1]).then_inc(y_square, 1)

            def batch(i, first, last):
                for f in range(FT + 1):
                    if f < FT:
                        n = M3 + f
                        act.wait_ge(bank_full, i * R + (n + 1))
                        act.activation(tanh[:, f % 2], ring[:, n % RING], ACT.Tanh, scale=0.5, bias=b1_half[:, f:f + 1])
                        act.activation(lin[:, f % 2], ring[:, n % RING], ACT.Identity,
                                       bias=b1[:, f:f + 1]).then_inc(h_lin, 1)
                    if f:
                        g = f - 1
                        act.wait_ge(h_mul, i * FT + (g + 1))
                        if g >= 3:
                            act.wait_ge(down_done, i * (FT - 1) + (g - 2))
                        elif not first and g < 2:
                            act.wait_ge(down_done, i * (FT - 1) + (g - 1))
                        elif not first:
                            act.wait_ge(sums_full, i * QT)
                        act.activation(hid_h[:, g % 3], act_f[:, g % 2], ACT.Copy).then_inc(h_hi, 1)
                    if f == 3 and not first:
                        squares_of(i - 1)
                if not last:
                    x_transposed(i + 1)

            x_transposed(0)
            act.wait_ge(const_in, 16 * 4)
            act.activation(w2_h[:], w2_raw[:], ACT.Copy, scale=0.5).then_inc(w_hi, 1)
            act.wait_ge(w_hi, 3)
            batch(0, True, False)
            with act.Fori(1, B - 1) as i:
                batch(i, False, False)
            batch(B - 1, False, True)
            squares_of(B - 1)

        @block.vector
        def _(dve):
            dve.wait_ge(w_hi, 1)
            dve.tensor_tensor(out=w1_l[:], in0=w1_raw[:], in1=w1_h[:], op=ALU.subtract).then_inc(w_lo, 1)
            dve.sem_inc(y_sum, QT)

            def x_transposed(i):
                for d in range(M3):
                    dve.wait_ge(xt_hi, i * M3 + (d + 1))
                    dve.tensor_tensor(out=at_l[:, d], in0=ring[:, d % RING], in1=at_h[:, d],
                                      op=ALU.subtract).then_inc(xt_lo, 1)

            def finish_part(i, f, first):
                if f in (1, 2):
                    if f == 1:
                        dve.wait_ge(a_kept, i * 16 + 16)
                        if not first:
                            dve.wait_ge(y_stored, i * 16)
                    for t in (2 * f - 2, 2 * f - 1):
                        dve.wait_ge(y_sum, i * QT + (QT + t + 1))
                        dve.tensor_tensor(out=y[:, t], in0=total[:, t], in1=a_res[:, t], op=ALU.add).then_inc(y_res, 1)
                if f == 4:
                    dve.wait_ge(y_square, i * QT + QT)
                    dve.tensor_scalar(out=spread[:, 0], in0=squares[:], scalar1=1.0 / D, scalar2=RMS_EPS,
                                      op0=ALU.mult, op1=ALU.add).then_inc(spread_made, 1)
                if f in (5, 6):
                    dve.wait_ge(rstd_ready, i * 2 + 1)
                    for t in (2 * f - 10, 2 * f - 9):
                        dve.scalar_tensor_tensor(out=y[:, t], in0=y[:, t], scalar=rstd[:, 0, t:t + 1], in1=al_row[:],
                                                 op0=ALU.mult, op1=ALU.mult).then_inc(y_scaled, 1)
                if f in (7, 8):
                    for t in (2 * f - 14, 2 * f - 13):
                        dve.wait_ge(x_gamma, i * QT + (t + 1))
                        dve.wait_ge(y_scaled, i * QT + (t + 1))
                        dve.tensor_tensor(out=y[:, t], in0=y[:, t], in1=x_res[:, t], op=ALU.add).then_inc(y_mixed, 1)
                if f in (9, 10):
                    for t in (2 * f - 18, 2 * f - 17):
                        dve.wait_ge(y_mixed, i * QT + (t + 1))
                        dve.bn_stats(stat[:, t], y[:, t]).then_inc(y_stat, 1)
                if f == 11:
                    for t in range(QT):
                        dve.wait_ge(w_lo, 2)
                        dve.wait_ge(y_stat, i * QT + (t + 1))
                        dve.bn_aggr(mean_var[:, t], stat[:, t]).then_inc(y_aggr, 1)
                    dve.wait_ge(y_aggr, i * QT + QT)
                    dve.tensor_scalar(out=spread[:, 1], in0=mean_var[:, :, 1], scalar1=LN_EPS, scalar2=None,
                                      op0=ALU.add).then_inc(spread_made, 1)
                if f == FT:
                    dve.wait_ge(rstd_ready, i * 2 + 2)
                    for t in range(QT):
                        dve.tensor_scalar(out=y[:, t], in0=y[:, t], scalar1=mean_var[:, t, 0:1],
                                          scalar2=rstd[:, 1, t:t + 1], op0=ALU.subtract, op1=ALU.mult).then_inc(y_ready, 1)

            def batch(i, first, second, last):
                for f in range(FT + 1):
                    if f < FT:
                        dve.wait_ge(h_lin, i * FT + (f + 1))
                        if f >= 2 or not first:
                            dve.wait_ge(h_lo, i * FT + (f - 1))
                        dve.scalar_tensor_tensor(out=act_f[:, f % 2], in0=tanh[:, f % 2], scalar=1.0, in1=lin[:, f % 2],
                                                 op0=ALU.add, op1=ALU.mult).then_inc(h_mul, 1)
                    if f:
                        g = f - 1
                        dve.wait_ge(h_hi, i * FT + (g + 1))
                        dve.tensor_tensor(out=hid_l[:, g % 3], in0=act_f[:, g % 2], in1=hid_h[:, g % 3],
                                          op=ALU.subtract).then_inc(h_lo, 1)
                    if not first and f < FT:
                        finish_part(i - 1, f, second)
                if not last:
                    x_transposed(i + 1)
                if not first:
                    finish_part(i - 1, FT, second)
                for t in range(QT):
                    if not first:
                        dve.wait_ge(y_res, i * QT - (QT - 1) + t)
                    dve.wait_ge(sums_full, i * QT + (t + 1))
                    dve.tensor_tensor(out=total[:, t], in0=sums[:, t, 0:D], in1=b2_row[:], op=ALU.add).then_inc(y_sum, 1)

            x_transposed(0)
            dve.wait_ge(w_hi, 3)
            dve.scalar_tensor_tensor(out=w2_l[:], in0=w2_raw[:], scalar=0.5, in1=w2_h[:],
                                     op0=ALU.mult, op1=ALU.subtract).then_inc(w_lo, 1)
            batch(0, True, False, False)
            batch(1, False, True, False)
            with dve.Fori(2, B - 1) as i:
                batch(i, False, False, False)
            batch(B - 1, False, False, True)
            for f in range(FT + 1):
                finish_part(B - 1, f, False)

        @block.tensor
        def _(pe):
            pe.wait_ge(first_in, 16 * 3)

            def x_transposed(i, first):
                pe.wait_ge(a_loaded, i * 16 + 16)
                for d in range(M3):
                    if not first:
                        pe.wait_ge(h_lin, i * FT - (M3 - 1 - d))
                    for t in range(QT):
                        last = pe.transpose(ring[:, d, t * P:(t + 1) * P], a_in[:, t, d * P:(d + 1) * P], ident[:])
                    last.then_inc(bank_full, 1)

            def batch(i, last_batch):
                def up(f):
                    n = M3 + f
                    if n < RING + M3 and n >= RING:
                        pe.wait_ge(xt_lo, i * M3 + (n - RING + 1))
                    elif n >= RING:
                        pe.wait_ge(h_lin, i * FT + (n - RING - M3 + 1))
                    bank, cols = ring[:, n % RING], slice(f * P, (f + 1) * P)
                    for d in range(M3):
                        if f == 0:
                            pe.wait_ge(xt_lo, i * M3 + (d + 1))
                        pe.matmul(bank, w1_h[:, d, cols], at_h[:, d], start=(d == 0), stop=False)
                        pe.matmul(bank, w1_h[:, d, cols], at_l[:, d], start=False, stop=False)
                        last = pe.matmul(bank, w1_l[:, d, cols], at_h[:, d], start=False, stop=(d == M3 - 1))
                    last.then_inc(bank_full, 1)

                def down(f):
                    pe.wait_ge(h_lo, i * FT + (f + 1))
                    if f == 0:
                        pe.wait_ge(w_lo, 2)
                    for t in range(QT):
                        if f == 0:
                            pe.wait_ge(y_sum, i * QT + (t + 1))
                        toks = slice(t * P, (t + 1) * P)
                        pe.matmul(sums[:, t, 0:D], hid_h[:, f % 3, toks], w2_h[:, f], start=(f == 0), stop=False)
                        pe.matmul(sums[:, t, 0:D], hid_h[:, f % 3, toks], w2_l[:, f], start=False, stop=False)
                        last = pe.matmul(sums[:, t, 0:D], hid_l[:, f % 3, toks], w2_h[:, f],
                                         start=False, stop=(f == FT - 1))
                        if f == FT - 1:
                            last.then_inc(sums_full, 1)
                    if f < FT - 1:
                        last.then_inc(down_done, 1)

                for f in range(FT + LAG):
                    if f < FT:
                        up(f)
                    if f >= LAG:
                        down(f - LAG)
                    if f == FT and not last_batch:
                        x_transposed(i + 1, False)

            x_transposed(0, True)
            pe.wait_ge(w_lo, 1)
            with pe.Fori(0, B - 1) as i:
                batch(i, False)
            batch(B - 1, True)


def build(nc, a, out, B, N, D):
    x1 = nc.dram_tensor("attended_dram", (B, N, D), F32, kind="Internal").ap()
    x2 = nc.dram_tensor("layer_0_dram", (B, N, D), F32, kind="Internal").ap()
    attention_layer(nc, Layer("a0", 8, 48, 2, 1.0, True, False), a["x"], a["adj"],
                    {k: a[f"L0_gnn_{n}"] for k, n in (("wq", "wq"), ("wk", "wk"), ("wv", "wv"), ("wo", "wo"), ("bq", "bq"),
                                                      ("bk", "bk"), ("bv", "bv"), ("bo", "bo"), ("alpha", "alpha1"),
                                                      ("gamma", "gamma1"))}, a["ident"], x1)
    feed_forward_layer(nc, x1, a["x"], {k: a[f"L0_gnn_{n}"] for k, n in (("w1", "w1"), ("w2", "w2"), ("b1", "b1"),
                                                                         ("b2", "b2"), ("alpha", "alpha2"),
                                                                         ("gamma", "gamma2"))}, a["ident"], x2)
    attention_layer(nc, Layer("a1", 12, 32, 1, 2.0, False, True), x2, a["adj"],
                    dict({k: a[f"L1_gnn_{n}"] for k, n in (("wq", "Wq"), ("wk", "Wk"), ("wv", "Wv"), ("wo", "Wo"),
                                                           ("bv", "bv"), ("bo", "bo"))}, head_mask=a["head_mask"]),
                    a["ident"], out)


COLUMNS = ("L0_gnn_bq", "L0_gnn_bk", "L0_gnn_b1")
BY_DIMENSION = ("L0_gnn_wq", "L0_gnn_bq", "L0_gnn_wk", "L0_gnn_bk")
BY_DIMENSION_1 = ("L1_gnn_Wq", "L1_gnn_Wk")
ROWS = ("L0_gnn_bo", "L0_gnn_b2", "L0_gnn_alpha1", "L0_gnn_gamma1", "L0_gnn_alpha2",
        "L0_gnn_gamma2", "L1_gnn_bv", "L1_gnn_bo")
TRANSPOSED = ("L1_gnn_Wq", "L1_gnn_Wk", "L1_gnn_Wv", "L1_gnn_Wo")


def kernel(**inputs):
    import numpy as _np
    import concourse.bacc as _bacc
    from concourse import mybir as _mybir
    from concourse.bass_utils import run_bass_kernel_spmd as _run

    nc = _bacc.Bacc("TRN2", target_bir_lowering=False, num_devices=1)
    inputs = dict(inputs, ident=_np.eye(P, dtype=_np.float32),
                  head_mask=_np.tile(_np.eye(4, dtype=_np.float32), (32, 1)))
    arrays, args = {}, {}
    for name, v in inputs.items():
        v = _np.asarray(v)
        if name in ROWS:
            v = _np.broadcast_to(v, (P, v.shape[0]))
        elif name in TRANSPOSED:
            v = v.T
        if name in BY_DIMENSION:
            v = _np.moveaxis(v.reshape(*v.shape[:-1], 8, 3, 16), -3, -1).reshape(v.shape)
        if name in BY_DIMENSION_1:
            v = v.reshape(-1, 3, 4, 32).swapaxes(-2, -1).reshape(v.shape)
        if name in COLUMNS:
            v = v.reshape(-1, P).T
        if name == "L0_gnn_bv":
            v = v.reshape(8, -1).T
        v = _np.ascontiguousarray(v)
        arrays[f"in_{name}_dram"] = v
        args[name] = nc.dram_tensor(f"in_{name}_dram", v.shape, _mybir.dt.from_np(v.dtype), kind="ExternalInput").ap()
    B, N, D = inputs["x"].shape
    out = nc.dram_tensor("out_0_dram", (B, N, D), _mybir.dt.float32, kind="ExternalOutput").ap()
    build(nc, args, out, B, N, D)
    r = _run(nc, [arrays], core_ids=[0])
    return r.results[0]["out_0_dram"]
```
